# Optimizing a Trainium2 kernel written in Bass

```python
import numpy as np
import jax
import jax.numpy as jnp

def _softmax(x, axis=-1):
    return jax.nn.softmax(x, axis=axis)

def _gelu(x):
    return jax.nn.gelu(x, approximate=True)

def _silu(x):
    return jax.nn.silu(x)

def _sigmoid(x):
    return jax.nn.sigmoid(x)

def _layernorm(x, axis=-1, eps=1e-05):
    m = jnp.mean(x, axis=axis, keepdims=True)
    v = jnp.var(x, axis=axis, keepdims=True)
    return (x - m) / jnp.sqrt(v + eps)

def _scatter_add(tgt, idx, src, axis=0):
    return tgt.at[idx].add(src)

def _segment_sum(src, seg, n):
    return jax.ops.segment_sum(src, seg, n)
kernel_name = 'mk_gps_d1_gnn_r8_ee1035'

def setup_inputs(seed: int=0):
    np.random.seed(seed)
    _w = jnp.asarray

    def _rec_inputs():
        import jax
        import jax.numpy as jnp
        _gk = jax.random.key(seed)
        x = -0.0003713 + 1 * jax.random.normal(jax.random.fold_in(_gk, 1), (6250, 256), jnp.float32)
        src = jax.random.randint(jax.random.fold_in(_gk, 2), (200000,), 0, 6250, jnp.int32)
        dst = jnp.minimum((6250 * jax.random.uniform(jax.random.fold_in(_gk, 3), (200000,)) ** 2.0).astype(jnp.int32), 49999)
        _o = jnp.argsort(dst, stable=True)
        src = src[_o]
        dst = dst[_o]
        return (x, src, dst)
    x, src, dst = _rec_inputs()

    def _L0_gnn_setup():
        import jax, jax.numpy as jnp
        import numpy as np
        N_NODES = 6250
        N_EDGES = 100000
        FEATURES = 256
        HEADS = 8
        HEAD_DIM = FEATURES // HEADS
        LAYERS = 3
        NEG_SLOPE_ATTN = 0.2
        NEG_SLOPE_ACT = 0.01

        def _gat_layer(x, W, al, ar, b, src, dst, apply_act):
            h = (x @ W).reshape(N_NODES, HEADS, HEAD_DIM)
            el = jnp.einsum('nhd,hd->nh', h, al)
            er = jnp.einsum('nhd,hd->nh', h, ar)
            e = jax.nn.leaky_relu(el[src] + er[dst], negative_slope=NEG_SLOPE_ATTN)
            m = jax.ops.segment_max(e, dst, num_segments=N_NODES)
            ex = jnp.exp(e - m[dst])
            s = jax.ops.segment_sum(ex, dst, num_segments=N_NODES)
            a = ex / s[dst]
            msg = h[src] * a[:, :, None]
            out = jax.ops.segment_sum(msg, dst, num_segments=N_NODES)
            out = out + b.reshape(1, HEADS, HEAD_DIM)
            out = out.reshape(N_NODES, FEATURES)
            if apply_act:
                out = jax.nn.leaky_relu(out, negative_slope=NEG_SLOPE_ACT)
            return out
        key = jax.random.key(seed)
        ks = jax.random.split(key, 7)
        x = jax.random.normal(ks[0], (N_NODES, FEATURES), dtype=jnp.float32)
        src = jax.random.randint(ks[1], (N_EDGES,), 0, N_NODES, dtype=jnp.int32)
        dst = jax.random.randint(ks[2], (N_EDGES,), 0, N_NODES, dtype=jnp.int32)
        W = jax.random.normal(ks[3], (LAYERS, FEATURES, FEATURES), dtype=jnp.float32) / np.sqrt(FEATURES)
        al = jax.random.normal(ks[4], (LAYERS, HEADS, HEAD_DIM), dtype=jnp.float32) * 0.1
        ar = jax.random.normal(ks[5], (LAYERS, HEADS, HEAD_DIM), dtype=jnp.float32) * 0.1
        b = jnp.zeros((LAYERS, FEATURES), dtype=jnp.float32)
        return {'x': x, 'src': src, 'dst': dst, 'W': W, 'al': al, 'ar': ar, 'b': b}
    _L0_gnn_all = _L0_gnn_setup()
    _L0_gnn_in = {k: v for k, v in _L0_gnn_all.items() if k in ('W', 'al', 'ar', 'b')}
    del _L0_gnn_all

    def _L0_mix_setup():
        import jax, jax.numpy as jnp
        import numpy as np
        NUM_HEADS = 8
        key = jax.random.key(seed)
        ks = jax.random.split(key, 5)
        B, N, C = (8, 2048, 256)
        x = jax.random.normal(ks[0], (B, N, C), dtype=jnp.float32)
        Wq = jax.random.normal(ks[1], (C, C), dtype=jnp.float32) * 0.02
        Wkv = jax.random.normal(ks[2], (2 * C, C), dtype=jnp.float32) * 0.02
        Wproj = jax.random.normal(ks[3], (C, C), dtype=jnp.float32) * 0.02
        bproj = jnp.zeros((C,), dtype=jnp.float32)
        return {'x': x, 'Wq': Wq, 'Wkv': Wkv, 'Wproj': Wproj, 'bproj': bproj}
    _L0_mix_all = _L0_mix_setup()
    _L0_mix_in = {k: v for k, v in _L0_mix_all.items() if k in ('Wq', 'Wkv', 'Wproj', 'bproj')}
    del _L0_mix_all

    def _L0_ffn_setup():
        import jax, jax.numpy as jnp
        import numpy as np
        E = 8
        K = 2
        D = 256
        H = 512
        DOUT = 256
        EPS = 1e-05
        key = jax.random.key(seed)
        ks = jax.random.split(key, 9)
        s = 0.02
        return {'x': jax.random.normal(ks[0], (4, 1024, D), jnp.float32), 'gamma': 1.0 + 0.05 * jax.random.normal(ks[1], (D,), jnp.float32), 'beta': 0.05 * jax.random.normal(ks[2], (D,), jnp.float32), 'Wr': 0.01 * jax.random.normal(ks[3], (D, E), jnp.float32), 'br': jnp.zeros((E,), jnp.float32), 'W1': s * jax.random.normal(ks[4], (E, D, H), jnp.float32), 'b1': s * jax.random.normal(ks[5], (E, H), jnp.float32), 'W2': s * jax.random.normal(ks[6], (E, H, DOUT), jnp.float32), 'b2': s * jax.random.normal(ks[7], (E, DOUT), jnp.float32)}
    _L0_ffn_all = _L0_ffn_setup()
    _L0_ffn_in = {k: v for k, v in _L0_ffn_all.items() if k in ('gamma', 'beta', 'Wr', 'br', 'W1', 'b1', 'W2', 'b2')}
    del _L0_ffn_all
    return {'x': x, 'src': src, 'dst': dst, 'L0_gnn_W': _L0_gnn_in['W'], 'L0_gnn_al': _L0_gnn_in['al'], 'L0_gnn_ar': _L0_gnn_in['ar'], 'L0_gnn_b': _L0_gnn_in['b'], 'L0_mix_Wq': _L0_mix_in['Wq'], 'L0_mix_Wkv': _L0_mix_in['Wkv'], 'L0_mix_Wproj': _L0_mix_in['Wproj'], 'L0_mix_bproj': _L0_mix_in['bproj'], 'L0_ffn_gamma': _L0_ffn_in['gamma'], 'L0_ffn_beta': _L0_ffn_in['beta'], 'L0_ffn_Wr': _L0_ffn_in['Wr'], 'L0_ffn_br': _L0_ffn_in['br'], 'L0_ffn_W1': _L0_ffn_in['W1'], 'L0_ffn_b1': _L0_ffn_in['b1'], 'L0_ffn_W2': _L0_ffn_in['W2'], 'L0_ffn_b2': _L0_ffn_in['b2']}

def reference(x, src, dst, L0_gnn_W, L0_gnn_al, L0_gnn_ar, L0_gnn_b, L0_mix_Wq, L0_mix_Wkv, L0_mix_Wproj, L0_mix_bproj, L0_ffn_gamma, L0_ffn_beta, L0_ffn_Wr, L0_ffn_br, L0_ffn_W1, L0_ffn_b1, L0_ffn_W2, L0_ffn_b2):
    import jax
    import jax.numpy as jnp

    def _L0_gnn_ref(x, src, dst, W, al, ar, b):
        import jax, jax.numpy as jnp
        import numpy as np
        N_NODES = 6250
        N_EDGES = 100000
        FEATURES = 256
        HEADS = 8
        HEAD_DIM = FEATURES // HEADS
        LAYERS = 3
        NEG_SLOPE_ATTN = 0.2
        NEG_SLOPE_ACT = 0.01

        def _gat_layer(x, W, al, ar, b, src, dst, apply_act):
            h = (x @ W).reshape(N_NODES, HEADS, HEAD_DIM)
            el = jnp.einsum('nhd,hd->nh', h, al)
            er = jnp.einsum('nhd,hd->nh', h, ar)
            e = jax.nn.leaky_relu(el[src] + er[dst], negative_slope=NEG_SLOPE_ATTN)
            m = jax.ops.segment_max(e, dst, num_segments=N_NODES)
            ex = jnp.exp(e - m[dst])
            s = jax.ops.segment_sum(ex, dst, num_segments=N_NODES)
            a = ex / s[dst]
            msg = h[src] * a[:, :, None]
            out = jax.ops.segment_sum(msg, dst, num_segments=N_NODES)
            out = out + b.reshape(1, HEADS, HEAD_DIM)
            out = out.reshape(N_NODES, FEATURES)
            if apply_act:
                out = jax.nn.leaky_relu(out, negative_slope=NEG_SLOPE_ACT)
            return out
        for i in range(LAYERS):
            x = _gat_layer(x, W[i], al[i], ar[i], b[i], src, dst, apply_act=i + 1 < LAYERS)
        return x

    def _L0_mix_ref(x, Wq, Wkv, Wproj, bproj):
        import jax, jax.numpy as jnp
        import numpy as np
        NUM_HEADS = 8
        B, N, C = x.shape
        h = NUM_HEADS
        d = C // h
        q = jnp.einsum('bnc,oc->bno', x, Wq).reshape(B, N, h, d).transpose(0, 2, 1, 3)
        kv = jnp.einsum('bnc,oc->bno', x, Wkv).reshape(B, N, 2, h, d)
        k = kv[:, :, 0].transpose(0, 2, 1, 3)
        v = kv[:, :, 1].transpose(0, 2, 1, 3)
        q = jax.nn.elu(q) + 1.0
        k = jax.nn.elu(k) + 1.0
        k_sum = k.sum(axis=2)
        D_inv = 1.0 / jnp.maximum(jnp.einsum('bhnd,bhd->bhn', q, k_sum), 1e-06)
        context = jnp.einsum('bhnd,bhne->bhde', k, v)
        attn = jnp.einsum('bhnd,bhde->bhne', q, context) * D_inv[..., None]
        out = attn.transpose(0, 2, 1, 3).reshape(B, N, C)
        out = jnp.einsum('bnc,oc->bno', out, Wproj) + bproj
        return out

    def _L0_ffn_ref(x, gamma, beta, Wr, br, W1, b1, W2, b2):
        import jax, jax.numpy as jnp
        import numpy as np
        E = 8
        K = 2
        D = 256
        H = 512
        DOUT = 256
        EPS = 1e-05
        mu = jnp.mean(x, axis=-1, keepdims=True)
        var = jnp.mean(jnp.square(x - mu), axis=-1, keepdims=True)
        xn = (x - mu) * jax.lax.rsqrt(var + EPS) * gamma + beta
        logits = jnp.einsum('bsd,de->bse', xn, Wr) + br
        top_vals, top_idx = jax.lax.top_k(logits, K)
        w = jax.nn.softmax(top_vals, axis=-1)
        w_full = jnp.einsum('bsk,bske->bse', w, jax.nn.one_hot(top_idx, E, dtype=w.dtype))
        y = jnp.zeros(x.shape[:-1] + (DOUT,), x.dtype)
        for e in range(E):
            h = jax.nn.gelu(jnp.einsum('bsd,dh->bsh', xn, W1[e]) + b1[e], approximate=False)
            y_e = jnp.einsum('bsh,hd->bsd', h, W2[e]) + b2[e]
            y = y + y_e * w_full[..., e, None]
        return y
    xn = _layernorm(x, axis=-1)
    x = x + _L0_gnn_ref(xn, src, dst, L0_gnn_W, L0_gnn_al, L0_gnn_ar, L0_gnn_b) + _L0_mix_ref(xn[None], L0_mix_Wq, L0_mix_Wkv, L0_mix_Wproj, L0_mix_bproj)[0]
    x = x + _L0_ffn_ref(_layernorm(x, axis=-1)[None], L0_ffn_gamma, L0_ffn_beta, L0_ffn_Wr, L0_ffn_br, L0_ffn_W1, L0_ffn_b1, L0_ffn_W2, L0_ffn_b2)[0]
    return x

_drawn_inputs = setup_inputs


def setup_inputs(seed=0):
    import zlib

    import numpy as np

    out = dict(_drawn_inputs(seed))
    spreads = {'L0_gnn_b': (0.0, 0.1), 'L0_mix_bproj': (0.0, 0.1), 'L0_ffn_br': (0.0, 0.1)}
    factors = {'L0_gnn_ar': 8.0,
     'L0_mix_Wq': 8.0,
     'L0_mix_Wkv': 8.0,
     'L0_mix_Wproj': 8.0,
     'L0_ffn_gamma': 6.063,
     'L0_ffn_beta': 4.857,
     'L0_ffn_b1': 8.0,
     'L0_ffn_b2': 4.323}
    for name, (base, spread) in spreads.items():
        noise = np.random.default_rng([zlib.crc32(name.encode()), seed]).standard_normal(out[name].shape)
        drawn = base * np.exp(spread * noise) if base else spread * noise
        out[name] = jnp.asarray(drawn.astype(out[name].dtype))
    for name, factor in factors.items():
        out[name] = (out[name] * factor).astype(out[name].dtype)
    return out
```

```python
import numpy as np
import concourse.bass as bass
from concourse import mybir
from contextlib import ExitStack

F32 = mybir.dt.float32
BF16 = mybir.dt.bfloat16
I32 = mybir.dt.int32
U32 = mybir.dt.uint32
ALU = mybir.AluOpType
ACT = mybir.ActivationFunctionType
AX = mybir.AxisListType

P = 128
N = 6250
E = 200000
C = 256
H = 8
D = C // H
LAYERS = 3
NT = -(-N // P)
NP = NT * P
CH = 4
SLOT = CH * P
RING = 4
CELL = 64
CELLS = -(-E // (CELL * P))
EP = CELLS * CELL * P
NO_NODE = 65536
BIG = 4096
EXT = C + 3 * H
MSG = H * (D + 1)
ROW = MSG + 2 * H
UV = 2 * H
EXPERTS = 8
HID = 512
HB = HID // P
SLOPE = 0.2
LEAK = 0.01
EPS = 1e-5
SAFE = 60.0
LOW = -1e30

K_ID, K_IOTA, K_BASE, K_VALID, K_CELL, K_CINV, K_TRI, K_LAST, K_MASK, K_ONE, K_NODE = (
    0, P, 2 * P, 2 * P + NT + 1, 2 * P + 2 * NT + 1, 2 * P + 2 * NT + 1 + CELLS, 2 * P + 2 * NT + 1 + 2 * CELLS,
    2 * P + 3 * NT + 1 + 2 * CELLS, 2 * P + 3 * NT + 2 + 2 * CELLS, 3 * P + 3 * NT + 2 + 2 * CELLS,
    4 * P + 3 * NT + 2 + 2 * CELLS)
K_ALL = K_NODE + NT + 1


def constants():
    k = np.zeros((P, K_ALL), np.float32)
    p = np.arange(P)[:, None]
    k[:, K_ID:K_IOTA] = np.eye(P)
    k[:, K_IOTA:K_BASE] = np.arange(P)
    k[:, K_BASE:K_VALID] = P * np.arange(NT + 1)
    k[:, K_VALID:K_CELL] = p + P * np.arange(NT) < N
    cell = p * CELLS + np.arange(CELLS)
    k[:, K_CELL:K_CINV] = cell + 1
    k[:, K_CINV:K_TRI] = BIG - cell
    k[:, K_TRI:K_LAST] = p < np.arange(NT)
    k[:, K_LAST] = np.arange(P) == NT - 1
    k[:, K_MASK:K_ONE] = p // D == np.arange(P) // D
    k[:, K_ONE:K_NODE] = 1
    k[:, K_NODE:] = p + P * np.arange(NT + 1)
    return k


def build(nc, a, out):
    es = ExitStack()
    with es:
        def sb(name, shape, dt=F32):
            return es.enter_context(nc.sbuf_tensor(name, shape, dt))

        def sem(name):
            return es.enter_context(nc.semaphore(name))

        table = [nc.dram_tensor(f"table{l}", (NP, ROW), F32).ap() for l in range(LAYERS)]
        xnT_d = nc.dram_tensor("xnT_d", (NT, P, C), F32).ap()
        qT_d = nc.dram_tensor("qT_d", (NT, P, C), F32).ap()
        ctl_d = nc.dram_tensor("ctl_d", (NT, 4), I32).ap()

        kc = sb("kc", [P, K_ALL])
        ident, iota = kc[:, K_ID:K_IOTA], kc[:, K_IOTA:K_BASE]
        ones = kc[:, K_ONE:K_ONE + P]
        node = kc[:, K_NODE:K_ALL]
        base, valid = kc[:, K_BASE:K_VALID], kc[:, K_VALID:K_CELL]
        res = sb("res", [P, NT, C])
        wext = sb("wext", [P, LAYERS, 2, EXT])
        b_bc = sb("b_bc", [P, LAYERS, C])
        bproj = sb("bproj", [P, C])
        wqT = sb("wqT", [P, 2, C])
        wkvT = sb("wkvT", [P, 2, 2 * C])
        wpT = sb("wpT", [P, 2, C])
        w1 = sb("w1", [P, EXPERTS, 2, HID])
        w2 = sb("w2", [P, EXPERTS, HB, C])
        b1 = sb("b1", [P, EXPERTS * HB])
        b2 = sb("b2", [EXPERTS, C])
        wr = sb("wr", [P, 2, EXPERTS])
        gb = sb("gb", [P, 4])
        br = sb("br", [P, EXPERTS])
        eler = sb("eler", [P, NT, 3 * H])
        uv = sb("uv", [P, NT, UV])
        uvb = sb("uvb", [P, 3, NT + 1, UV], BF16)
        meta = sb("meta", [P, RING, CH, 2], I32)
        dstb = sb("dstb", [P, RING, SLOT], I32)
        gat = sb("gat", [P, RING, CH, ROW])
        dl = sb("dl", [P, CH])
        sel = sb("sel", [P, CH, P])
        selT = sb("selT", [P, CH, P], BF16)
        lg2 = sb("lg2", [P, CH, UV])
        lg = sb("lg", [P, CH, H])
        ex = sb("ex", [P, CH, H])
        msg = sb("msg", [P, CH, MSG])
        zb = sb("zb", [P, MSG], BF16)
        ctl = sb("ctl", [1, NT, 4], I32)
        small = sb("small", [P, 512])
        ismall = sb("ismall", [P, 64], I32)
        mv = sb("mv", [P, NT, 2])
        mv2 = sb("mv2", [P, NT, 2])
        bst = sb("bst", [P, 7, 6])
        bag = sb("bag", [P, 7, 2])
        rstd = sb("rstd", [P, NT])
        rstd2 = sb("rstd2", [P, NT])
        xn = sb("xn", [P, 2, C])
        xT = sb("xT", [P, 2, 2, P])
        hrow = sb("hrow", [P, 2, ROW])
        rec = sb("rec", [P, H])
        region = sb("region", [P, 3456])
        dcell = region[:, 0:CELLS * CELL].bitcast(I32).rearrange("p (a b) -> p a b", b=CELL)
        albc = region[:, 1600:1600 + LAYERS * C].rearrange("p (l c) -> p l c", c=C)
        arbc = region[:, 2400:2400 + LAYERS * C].rearrange("p (l c) -> p l c", c=C)
        hit = gat[:, :, :, :].rearrange("p a b c -> p (a b c)")
        xnTs = region[:, 0:256].rearrange("p (b n) -> p b n", b=2)
        neg = region[:, 256:768]
        epos = region[:, 768:1280]
        kq = region[:, 1280:1792]
        vx = region[:, 1792:1792 + C + 1]
        ctxm = region[:, 2060:2316].rearrange("p (b n) -> p b n", b=2)
        ksx = region[:, 2316:2572].rearrange("p (b n) -> p b n", b=2)
        qTs = region[:, 2572:2828].rearrange("p (b n) -> p b n", b=2)
        den = region[:, 2828:3084]
        ats = region[:, 3084:3340]
        zt = region[:, 0:7 * C].rearrange("p (j c) -> p j c", j=7)
        gT = region[:, 0:1024].rearrange("p (s b n) -> p s b n", s=2, b=HB)
        yacc = region[:, 1024:1536].rearrange("p (s c) -> p s c", s=2)
        rt = region[:, 1536:1700]
        wT = region[0:EXPERTS, 1700:1828]
        mi8 = region[:, 1830:1838].bitcast(U32)

        def by_head(x):
            return x.rearrange("p (h d) -> p h d", h=H)

        bank = [es.enter_context(nc.psum_tensor(f"bank{i}", [P, 512], F32)) for i in range(8)]
        acc = bank[0]
        uv_p = bank[2]
        tp = bank[3]
        hp = bank[4]

        x_in, k_in, w_in, d_in, late_in = map(sem, ("x_in", "k_in", "w_in", "d_in", "late_in"))
        ext_ready, var_ready, std_ready, flags_ready, flagsT_ready, slots_ready, sums_ready, ctl_ready = map(
            sem, ("ext_ready", "var_ready", "std_ready", "flags_ready", "flagsT_ready", "slots_ready", "sums_ready",
                  "ctl_ready"))
        ctl_out, ctl_in, zeros_ready = sem("ctl_out"), sem("ctl_in"), sem("zeros_ready")
        xn_ready, xn_free, xT_psum, xT_ready = map(sem, ("xn_ready", "xn_free", "xT_psum", "xT_ready"))
        xT_out = [sem("xT_out0"), sem("xT_out1")]
        h_done, hp_free = ([sem(f"{n}{l}") for l in range(LAYERS)] for n in ("h_done", "hp_free"))
        row_out = [[sem(f"row_out{l}_{b}") for b in range(2)] for l in range(LAYERS)]
        (uvb_ready, extremes, extremesT, spread, spread_done, meta_in, dst_in, slot_taken, meta_ready, gathered, slot_free, sel_ready, selT_ready, uv_ready, logit_ready, ex_ready, msg_ready, agg_done, acc_done, acc_free, xo_ready, xoT_psum,
         xoT_ready) = (
            [sem(f"{n}{l}") for l in range(LAYERS)] for n in (
                "uvb_ready", "extremes", "extremesT", "spread", "spread_done", "meta_in", "dst_in", "slot_taken", "meta_ready", "gathered", "slot_free",
                "sel_ready", "selT_ready", "uv_ready", "logit_ready", "ex_ready", "msg_ready",
                "agg_done", "acc_done", "acc_free", "xo_ready", "xoT_psum", "xoT_ready"))
        slot_in = [[sem(f"slot_in{l}_{r}") for r in range(RING)] for l in range(LAYERS)]
        xnT_in, mix_psum, neg_ready, exp_ready, v_ready, kq_ready, mix_free, q_out, ctx_done, ctx_ready = map(
            sem, ("xnT_in", "mix_psum", "neg_ready", "exp_ready", "v_ready", "kq_ready", "mix_free", "q_out",
                  "ctx_done", "ctx_ready"))
        qT_in, at_psum, ats_ready, o_psum, o_free = map(sem, ("qT_in", "at_psum", "ats_ready", "o_psum", "o_free"))
        f_var, f_std, f_var2, f_std2 = map(sem, ("f_var", "f_std", "f_var2", "f_std2"))
        f_xn, f_tp, f_xT, f_lg, f_d, f_t, f_w, f_wT_p, f_wT, f_b2, f_h, f_g, f_y, f_yd, f_acc = map(
            sem, ("f_xn", "f_tp", "f_xT", "f_lg", "f_d", "f_t", "f_w", "f_wT_p", "f_wT", "f_b2", "f_h", "f_g",
                  "f_y", "f_yd", "f_acc"))
        f_out = [sem("f_out0"), sem("f_out1")]
        ROWS = [[16 * (NT // 2 + 2), 16 * (NT // 2 + 1)]] + [[16 * (NT + 1), 0]] * (LAYERS - 1)
        LATE = 12
        FRONT, BACK = range(0, CH // 2), range(CH // 2, CH)

        block = es.enter_context(nc.Block())


        def tile_ctl(eng, T):
            n = eng.value_load(ctl[0:1, bass.ds(T, 1), 1:2].rearrange("a b c -> a (b c)"), min_val=1, max_val=SLOTS_MAX)
            before = eng.value_load(ctl[0:1, bass.ds(T, 1), 2:3].rearrange("a b c -> a (b c)"), min_val=0, max_val=TOTAL_MAX)
            return n, before

        def next_tile(T, k, n):
            return nc.s_assert_within(T + (k + 1) // n, 0, NT, skip_runtime_bounds_check_because="k < n")

        SLOTS_MAX = EP // SLOT + RING
        TOTAL_MAX = NT * SLOTS_MAX

        @block.sync
        def _(sp):
            sp.dma_start(dcell, a["dst"].rearrange("(p a b) -> p a b", p=P, b=CELL)).then_inc(d_in, 16)
            sp.dma_start(kc[:], a["consts"]).then_inc(k_in, 16)
            sp.dma_start(res[:], a["x"].rearrange("(t p) c -> p t c", p=P)).then_inc(x_in, 16)
            for l in range(LAYERS):
                sp.dma_start(wext[:, l, :, 0:C], a["W"][l].rearrange("(k p) c -> p k c", p=P)).then_inc(w_in, 16)
            sp.dma_start(albc, a["al"].rearrange("(a l) c -> a l c", a=1).to_broadcast([P, LAYERS, C])).then_inc(w_in, 16)
            sp.dma_start(arbc, a["ar"].rearrange("(a l) c -> a l c", a=1).to_broadcast([P, LAYERS, C])).then_inc(w_in, 16)
            for dst, src in ((b_bc[:], a["b"].rearrange("(a l) c -> a l c", a=1).to_broadcast([P, LAYERS, C])),
                             (bproj[:], a["bproj"].rearrange("(a c) -> a c", a=1).to_broadcast([P, C])),
                             (br[:], a["br"].rearrange("(a c) -> a c", a=1).to_broadcast([P, EXPERTS])),
                             (wqT[:], a["wqT"].rearrange("(k p) c -> p k c", p=P)),
                             (wkvT[:], a["wkvT"].rearrange("(k p) c -> p k c", p=P)),
                             (wpT[:], a["wpT"].rearrange("(k p) c -> p k c", p=P)),
                             (w1[:, :, :, :], a["W1"].rearrange("e (k p) h -> p e k h", p=P)),
                             (w2[:, :, :, :], a["W2"].rearrange("e (k p) c -> p e k c", p=P)),
                             (b1[:], a["b1"]), (b2[:], a["b2"]), (gb[:], a["gb"]),
                             (wr[:], a["Wr"].rearrange("(k p) c -> p k c", p=P))):
                sp.dma_start(dst, src).then_inc(late_in, 16)
            sp.wait_ge(ctl_ready, 1)
            sp.dma_start(ctl_d, ismall[0:NT, 4:8]).then_inc(ctl_out, 16)
            sp.wait_ge(ctl_out, 16)
            sp.dma_start(ctl[:], ctl_d.rearrange("(a t) c -> a t c", a=1)).then_inc(ctl_in, 16)
            sp.wait_ge(ctl_in, 16)

            for l in range(LAYERS):
                def load_slot(edge, n):
                    sp.wait_ge(slot_free[l], n + 1)
                    sp.sem_inc(slot_taken[l], 1)
                    sp.dma_start(meta[:, bass.ds(n % RING, 1), :, :].rearrange("p a c w -> p (a c w)"),
                                 a["edges"][bass.ds(2 * edge, SLOT * 2)].rearrange("(p f) -> p f", p=P)).then_inc(meta_in[l], 16)
                    sp.dma_start(dstb[:, bass.ds(n % RING, 1), :].rearrange("p a e -> p (a e)"),
                                 a["dst"][bass.ds(edge, SLOT)].rearrange("(a e) -> a e", a=1).to_broadcast([P, SLOT])
                                 ).then_inc(dst_in[l], 16)
                    sp.wait_ge(meta_in[l], 16 * (n + 1))
                    sp.wait_ge(dst_in[l], 16 * (n + 1))
                    sp.sem_inc(meta_ready[l], 1)

                with sp.Fori(0, NT) as T:
                    n_T, before = tile_ctl(sp, T)
                    start = sp.value_load(ctl[0:1, bass.ds(T, 1), 0:1].rearrange("a b c -> a (b c)"), min_val=0, max_val=EP)
                    with sp.Fori(0, n_T) as k:
                        edge = nc.s_assert_within(start + k * SLOT, 0, EP - SLOT,
                                                  skip_runtime_bounds_check_because="a tile's slots end inside the padding")
                        load_slot(edge, before + k)
                rounds = sp.value_load(ctl[0:1, 0:1, 3:4].rearrange("a b c -> a (b c)"), min_val=12, max_val=TOTAL_MAX // RING)
                load_slot(0, rounds * RING + RING)

            for b in range(2):
                sp.sem_inc(f_out[b], 16)

            def store(T, b):
                sp.wait_ge(f_acc, T + 1)
                sp.dma_start(out[bass.ds(T * P, P), :], yacc[:, b, :]).then_inc(f_out[b], 16)

            store(0, 0)
            with sp.Fori(0, NT // 2) as i:
                store(2 * i + 1, 1)
                store(2 * i + 2, 0)
            for b in range(2):
                sp.wait_ge(f_out[b], ROWS[0][b])

        @block.gpsimd
        def _(pool):
            pool.memset(zb[:], 0.0).then_inc(zeros_ready, 1)
            pool.memset(hrow[:], 1.0).then_inc(zeros_ready, 1)
            pool.wait_ge(ctl_in, 16)
            rounds = pool.value_load(ctl[0:1, 0:1, 3:4].rearrange("a b c -> a (b c)"), min_val=12, max_val=TOTAL_MAX // RING)
            for l in range(LAYERS):
                def gather(n, r):
                    for c in range(CH):
                        pool.indirect_dma_start(gat[:, r, c, :], None, table[l],
                                                bass.IndirectOffsetOnAxis(meta[:, r, c, 0:1].bitcast(U32), 0)
                                                ).then_inc(slot_in[l][r], 16)

                def ready(n):
                    pool.wait_ge(slot_free[l], n + 1)
                    pool.wait_ge(meta_ready[l], n + 1)

                def announce(r, turn):
                    pool.wait_ge(slot_in[l][r], 16 * CH * turn)
                    pool.sem_inc(gathered[l], 1)

                for b in range(2):
                    if ROWS[l][b]:
                        pool.wait_ge(row_out[l][b], ROWS[l][b])
                for n in range(2):
                    ready(n)
                    gather(n, n)
                with pool.Fori(0, rounds) as i:
                    for j in range(RING):
                        n = RING * i + 2 + j
                        ready(n)
                        announce(j, i + 1)
                        gather(n, (2 + j) % RING)
                for j in range(2):
                    ready(RING * rounds + 2 + j)
                    announce(j, rounds + 1)
                    gather(RING * rounds + 2 + j, 2 + j)
                for j in range(2, RING):
                    announce(j, rounds + 1)

        @block.scalar
        def _(act):
            def row_copy(T, b, l, turn):
                act.wait_ge(row_out[l][b], 16 * turn)
                act.wait_ge(h_done[l], T + 1)
                act.activation(by_head(hrow[:, b, 0:MSG])[:, :, 0:D], hp[:, 0:C].rearrange("p (h d) -> p h d", h=H), ACT.Copy)
                act.activation(hrow[:, b, MSG:ROW], hp[:, C:C + UV], ACT.Copy)
                act.activation(eler[:, bass.ds(T, 1), :].rearrange("p a c -> p (a c)"), hp[:, C:EXT], ACT.Copy).then_inc(hp_free[l], 1)
                act.drain()
                act.dma_start(table[l][bass.ds(T * P, P), :], hrow[:, b, :]).then_inc(row_out[l][b], 16)

            for b in range(2):
                act.sem_inc(row_out[0][b], 16)
                act.sem_inc(xT_out[b], 16)
            act.sem_inc(hp_free[0], 1)
            act.wait_ge(zeros_ready, 2)
            act.wait_ge(var_ready, 1)
            act.activation(rstd[:], rstd[:], ACT.Sqrt).then_inc(std_ready, 1)

            def first(T, b, turn):
                act.wait_ge(xT_out[b], 16 * turn)
                act.wait_ge(xT_psum, T + 1)
                act.activation(xT[:, b, :, :].rearrange("p a b -> p (a b)"), tp[:, 0:C], ACT.Copy).then_inc(xT_ready, 1)
                act.wait_ge(xT_ready, T + 1)
                act.dma_start(xnT_d[bass.ds(T, 1), :, :].rearrange("a p c -> (a p) c"),
                              xT[:, b, :, :].rearrange("p a b -> p (a b)")).then_inc(xT_out[b], 16)
                row_copy(T, b, 0, turn)

            first(0, 0, 1)
            with act.Fori(0, NT // 2) as i:
                first(2 * i + 1, 1, i + 1)
                first(2 * i + 2, 0, i + 2)
            for b in range(2):
                act.wait_ge(xT_out[b], ROWS[0][b])

            for l in range(LAYERS):
                if l + 1 < LAYERS:
                    act.sem_inc(row_out[l + 1][0], 16)
                    act.sem_inc(hp_free[l + 1], 1)
                if l == 0:
                    act.sem_inc(q_out, 16)

                act.wait_ge(ctl_in, 16)
                with act.Fori(0, NT) as T:
                    n_T, before = tile_ctl(act, T)
                    if l == 0:
                        act.dma_start(xnTs.rearrange("p b n -> p (b n)"),
                                      xnT_d[bass.ds(T, 1), :, :].rearrange("a p c -> (a p) c")).then_inc(xnT_in, 16)
                    if l == 1:
                        act.dma_start(qTs.rearrange("p b n -> p (b n)"),
                                      qT_d[bass.ds(T, 1), :, :].rearrange("a p c -> (a p) c")).then_inc(qT_in, 16)
                    with act.Fori(0, n_T) as k:
                        n = before + k
                        act.wait_ge(logit_ready[l], n + 1)
                        act.activation(ex[:], lg[:], ACT.Exp).then_inc(ex_ready[l], 1)
                    if l == 0:
                        act.wait_ge(mix_psum, T + 1)
                        act.wait_ge(mix_free, T + 1)
                        act.activation(vx[:, 0:C], bank[5][:, C:2 * C], ACT.Copy).then_inc(v_ready, 1)
                        act.wait_ge(neg_ready, T + 1)
                        act.activation(epos, neg, ACT.Exp).then_inc(exp_ready, 1)
                        act.wait_ge(kq_ready, T + 1)
                        act.dma_start(qT_d[bass.ds(T, 1), :, :].rearrange("a p c -> (a p) c"), kq[:, C:2 * C]).then_inc(q_out, 16)
                    if l + 1 < LAYERS:
                        act.wait_ge(xoT_psum[l], T + 1)
                        act.activation(xT[:, 0, :, :].rearrange("p a b -> p (a b)"), tp[:, 0:C], ACT.Copy).then_inc(xoT_ready[l], 1)
                        row_copy(T, 0, l + 1, T + 1)
                if l == 0:
                    act.wait_ge(q_out, 16 * (NT + 1))

            act.wait_ge(late_in, 16 * LATE)
            act.wait_ge(f_var, 1)
            act.activation(rstd[:], rstd[:], ACT.Sqrt).then_inc(f_std, 1)
            act.wait_ge(f_var2, 1)
            act.activation(rstd2[:], rstd2[:], ACT.Sqrt).then_inc(f_std2, 1)
            with act.Fori(0, NT) as T:
                act.wait_ge(f_tp, T + 1)
                for c in range(2):
                    act.activation(xT[:, 0, c, :], tp[:, c * P:(c + 1) * P], ACT.Identity,
                                   bias=gb[:, 2 + c:3 + c], scale=gb[:, c:c + 1]).then_inc(f_xT, 1)
                act.wait_ge(f_d, T + 1)
                act.activation(rt[:, 40:41], rt[:, 24:25], ACT.Tanh, scale=0.5).then_inc(f_t, 1)
                for e in range(EXPERTS):
                    if e == 1:
                        act.wait_ge(f_wT_p, T + 1)
                        act.activation(wT, hp[0:EXPERTS, 128:256], ACT.Copy).then_inc(f_wT, 1)
                    act.wait_ge(f_h, EXPERTS * T + e + 1)
                    for k in range(HB):
                        last = act.activation(gT[:, e % 2, k, :], bank[5 + e % 2][:, k * P:(k + 1) * P], ACT.Gelu,
                                              bias=b1[:, e * HB + k:e * HB + k + 1])
                    last.then_inc(f_g, 1)

        @block.vector
        def _(dve):
            dve_v = nc.vector

            dve.wait_ge(w_in, 16 * (LAYERS + 2))
            hv = hit[:, 0:LAYERS * 2 * C].rearrange("p (l k c) -> p l k c", l=LAYERS, k=2)
            hr = hit[:, 0:LAYERS * 2 * C].rearrange("p (l h d) -> p l h d", l=LAYERS * 2, h=H)
            wflat = wext[:, :, :, :].rearrange("p l k c -> p (l k) c")
            for src, at in ((albc, C), (arbc, C + UV)):
                for l in range(LAYERS):
                    dve_v.tensor_tensor(hv[:, l], wext[:, l, :, 0:C], src[:, l:l + 1, :].to_broadcast([P, 2, C]), ALU.mult)
                dve.drain()
                dve_v.tensor_reduce(wflat[:, :, at:at + H], hr, AX.X, ALU.add)
                dve.drain()
            dve_v.tensor_scalar(wflat[:, :, C + H:C + UV], wflat[:, :, C:C + H], SLOPE, None, ALU.mult).then_inc(ext_ready, 1)

            def norm_stats(src, to):
                with dve.Fori(0, NT // 7) as i:
                    for j in range(7):
                        dve_v.bn_stats(bst[:, j, :], src(i, j))
                    dve.drain()
                    for j in range(7):
                        dve_v.bn_aggr(bag[:, j, :], bst[:, j, :])
                    dve.drain()
                    dve_v.tensor_copy(to[:, bass.ds(7 * i, 7), :], bag[:])
                    dve.drain()

            def res_tile(T):
                return res[:, bass.ds(T, 1), :].rearrange("p a c -> p (a c)")

            dve.wait_ge(x_in, 16)
            dve.wait_ge(k_in, 16)
            norm_stats(lambda i, j: res_tile(7 * i + j), mv)
            dve_v.tensor_scalar(rstd[:], mv[:, :, 1], EPS, None, ALU.add).then_inc(var_ready, 1)

            dve.wait_ge(d_in, 16)
            lo, hi = small[:, 0:CELLS], small[:, 32:32 + CELLS]
            dve_v.tensor_reduce(lo, dcell, AX.X, ALU.min)
            dve_v.tensor_reduce(hi, dcell, AX.X, ALU.max)
            top = small[:, 64:64 + NT]
            dve_v.tensor_scalar(top, base[:, 0:NT], float(P - 1), None, ALU.add)
            dve.drain()
            NC = NT * CELLS
            h1 = hit[:, 0:NC].rearrange("p (t c) -> p t c", t=NT)
            h2 = hit[:, NC:2 * NC].rearrange("p (t c) -> p t c", t=NT)
            cells = [P, NT, CELLS]
            dve_v.tensor_tensor(h1, lo.unsqueeze(1).to_broadcast(cells), top.unsqueeze(2).to_broadcast(cells), ALU.is_le)
            dve_v.tensor_tensor(h2, hi.unsqueeze(1).to_broadcast(cells), base[:, 0:NT].unsqueeze(2).to_broadcast(cells), ALU.is_ge)
            dve.drain()
            dve_v.tensor_tensor(h1, h1, h2, ALU.mult)
            dve.drain()
            fl = small[:, 128:128 + 2 * NT].rearrange("p (w t) -> p w t", w=2)
            for w, at in ((0, K_CELL), (1, K_CINV)):
                dve_v.tensor_tensor(h2, h1, kc[:, at:at + CELLS].unsqueeze(1).to_broadcast(cells), ALU.mult)
                dve.drain()
                dve_v.tensor_reduce(fl[:, w, :], h2, AX.X, ALU.max)
                dve.drain()
            dve.sem_inc(flags_ready, 1)
            dve.wait_ge(flagsT_ready, 1)
            lf = small[:, 240:244]
            dve_v.tensor_reduce(lf[0:NT, 0:1], tp[0:NT, 0:P], AX.X, ALU.max)
            dve_v.tensor_reduce(lf[0:NT, 1:2], tp[0:NT, P:2 * P], AX.X, ALU.max)
            dve.drain()
            dve_v.tensor_scalar(lf[0:NT, 0:1], lf[0:NT, 0:1], 1.0, None, ALU.max)
            dve_v.tensor_scalar(lf[0:NT, 1:2], lf[0:NT, 1:2], -1.0, float(BIG), ALU.mult, ALU.add)
            dve.drain()
            dve_v.tensor_scalar(lf[0:NT, 2:3], lf[0:NT, 0:1], -1.0, None, ALU.add)
            dve.drain()
            dve_v.tensor_tensor(lf[0:NT, 1:2], lf[0:NT, 1:2], lf[0:NT, 2:3], ALU.min)
            dve.drain()
            per = SLOT // CELL
            dve_v.tensor_tensor(lf[0:NT, 2:3], lf[0:NT, 0:1], lf[0:NT, 1:2], ALU.subtract)
            dve.drain()
            dve_v.tensor_scalar(ismall[0:NT, 0:1], lf[0:NT, 2:3], float(per - 1), None, ALU.add)
            dve_v.tensor_scalar(ismall[0:NT, 4:5], lf[0:NT, 1:2], float(CELL), None, ALU.mult)
            dve.drain()
            dve_v.tensor_scalar(ismall[0:NT, 1:2], ismall[0:NT, 0:1], per.bit_length() - 1, None, ALU.logical_shift_right)
            dve.drain()
            dve_v.tensor_copy(lf[0:NT, 3:4], ismall[0:NT, 1:2]).then_inc(slots_ready, 1)
            dve.wait_ge(sums_ready, 1)
            dve_v.tensor_copy(ismall[0:NT, 6:7], tp[0:NT, 256:257])
            dve_v.tensor_scalar(ismall[0:NT, 2:3], tp[0:NT, 257:258], -1.0, float(RING * TOTAL_MAX), ALU.mult, ALU.add)
            dve_v.tensor_scalar(ismall[0:NT, 3:4], tp[0:NT, 257:258], -1.0, None, ALU.add)
            dve.drain()
            dve_v.tensor_scalar(ismall[0:NT, 2:3], ismall[0:NT, 2:3], RING - 1, None, ALU.bitwise_and)
            dve_v.tensor_scalar(ismall[0:NT, 7:8], ismall[0:NT, 3:4], RING.bit_length() - 1, None, ALU.logical_shift_right)
            dve.drain()
            dve_v.tensor_copy(lf[0:NT, 0:1], ismall[0:NT, 2:3])
            dve.drain()
            dve_v.tensor_tensor(lf[0:NT, 0:1], lf[0:NT, 0:1], kc[0:NT, K_LAST:K_LAST + 1], ALU.mult)
            dve.drain()
            dve_v.tensor_tensor(ismall[0:NT, 5:6], lf[0:NT, 0:1], lf[0:NT, 3:4], ALU.add).then_inc(ctl_ready, 1)

            dve.wait_ge(std_ready, 1)
            dve_v.reciprocal(rstd[:], rstd[:])
            dve.drain()

            def first(T, b):
                dve.wait_ge(xn_free, T + 1)
                dve_v.tensor_scalar(xn[:, b, :], res_tile(T), mv[:, bass.ds(T, 1), 0:1].rearrange("p a b -> p (a b)"),
                                    rstd[:, bass.ds(T, 1)], ALU.subtract, ALU.mult).then_inc(xn_ready, 1)

            first(0, 0)
            with dve.Fori(0, NT // 2) as i:
                first(2 * i + 1, 1)
                first(2 * i + 2, 0)

            def reference_logits(l):
                ext = eler[:, :, :].rearrange("p t c -> p c t")
                dve_v.tensor_reduce(small[:, 0:H], ext[:, 0:H, :], AX.X, ALU.max)
                dve_v.tensor_reduce(small[:, H:2 * H], ext[:, 0:H, :], AX.X, ALU.min)
                dve.drain()
                dve_v.tensor_scalar(small[:, H:2 * H], small[:, H:2 * H], -1.0, None, ALU.mult)
                dve.drain()
                dve.sem_inc(extremes[l], 1)
                dve.wait_ge(extremesT[l], 1)
                dve_v.tensor_reduce(small[0:2 * H, 16:17], tp[0:2 * H, 0:P], AX.X, ALU.max)
                dve.drain()
                dve_v.tensor_scalar(small[0:2 * H, 32:48], ident[0:2 * H, 0:2 * H], small[0:2 * H, 16:17], None, ALU.mult)
                dve.drain()
                dve.sem_inc(spread[l], 1)
                dve.wait_ge(spread_done[l], 1)
                dve_v.tensor_copy(small[:, 64:80], tp[:, 0:2 * H])
                dve.drain()
                er = eler[:, :, 2 * H:3 * H]
                u, v = uv[:, :, 0:H], uv[:, :, H:UV]
                hb = [P, NT, H]
                dve_v.tensor_tensor(u, er, small[:, 64:64 + H].unsqueeze(1).to_broadcast(hb), ALU.add)
                dve.drain()
                dve_v.tensor_scalar(v, u, SLOPE, None, ALU.mult)
                dve.drain()
                c = hit[:, 0:NT * H].rearrange("p (t h) -> p t h", h=H)
                dve_v.tensor_tensor(c, u, v, ALU.max)
                dve.drain()
                dve_v.tensor_tensor(u, er, c, ALU.subtract)
                dve_v.tensor_scalar(v, er, SLOPE, None, ALU.mult)
                dve.drain()
                dve_v.tensor_tensor(v, v, c, ALU.subtract)
                dve.drain()
                flat = uv[:, :, :].rearrange("p t c -> p (t c)")
                rest = hit[:, 1024:1024 + NT * UV]
                part = [uvb[:, i, 0:NT, :].rearrange("p t c -> p (t c)") for i in range(3)]
                dve_v.tensor_copy(part[0], flat)
                dve.drain()
                dve_v.tensor_tensor(rest, flat, part[0], ALU.subtract)
                dve.drain()
                dve_v.tensor_copy(part[1], rest)
                dve.drain()
                dve_v.tensor_tensor(rest, rest, part[1], ALU.subtract)
                dve.drain()
                dve_v.tensor_copy(part[2], rest).then_inc(uvb_ready[l], 1)

            dve_v.memset(uvb[:, :, NT, :], 0.0)
            for l in range(LAYERS):
                dve.wait_ge(hp_free[l], NT + 1)
                reference_logits(l)
                dve.drain()
                dve.sem_inc(slot_free[l], RING - 1)
                dve.sem_inc(acc_free[l], 1)
                dve.wait_ge(ctl_in, 16)
                if l == 1:
                    dve.sem_inc(o_free, 1)
                if l == 0:
                    dve.wait_ge(late_in, 16 * LATE)
                    dve_v.tensor_tensor(b_bc[:, 2, :], b_bc[:, 2, :], bproj[:], ALU.add)

                def selectT(n, T):
                    dve.wait_ge(meta_ready[l], n + 1)
                    dve_v.tensor_scalar(selT[:, :, :], dstb[:, bass.ds(n % RING, 1), :].rearrange("p a (e c) -> p (a c) e", c=CH),
                                        node[:, bass.ds(T, 1)], None, ALU.is_equal).then_inc(selT_ready[l], 1)

                def place(n, T):
                    dve.wait_ge(meta_ready[l], n + 1)
                    if not isinstance(n, int):
                        dve.wait_ge(sel_ready[l], CH * n)
                    dve_v.tensor_scalar(dl[:], meta[:, bass.ds(n % RING, 1), :, 1:2].rearrange("p a c w -> p (a c w)"),
                                        base[:, bass.ds(T, 1)], None, ALU.subtract).then_inc(slot_free[l], 1)
                    dve.drain()

                def select(n, chunks):
                    for c in chunks:
                        if not isinstance(n, int):
                            dve.wait_ge(agg_done[l], CH * n + c + 1)
                        dve_v.tensor_scalar(sel[:, c, :], iota, dl[:, c:c + 1], None, ALU.is_equal).then_inc(sel_ready[l], 1)

                selectT(0, 0)
                place(0, 0)
                select(0, FRONT)
                dve.sem_inc(agg_done[l], CH)
                with dve.Fori(0, NT) as T:
                    n_T, before = tile_ctl(dve, T)
                    with dve.Fori(0, n_T) as k:
                        n = before + k
                        rows = gat[:, bass.ds(n % RING, 1), :, :].rearrange("p a c w -> p (a c) w")
                        dve.wait_ge(uv_ready[l], n + 1)
                        dve.wait_ge(gathered[l], n + 1)
                        dve_v.tensor_tensor(lg2[:], rows[:, :, MSG:ROW],
                                            uv_p[:, 0:CH * UV].rearrange("p (c w) -> p c w", w=UV), ALU.add)
                        dve.drain()
                        dve_v.tensor_tensor(lg[:], lg2[:, :, 0:H], lg2[:, :, H:UV], ALU.max).then_inc(logit_ready[l], 1)
                        selectT(n + 1, next_tile(T, k, n_T))
                        select(n, BACK)
                        dve.wait_ge(ex_ready[l], n + 1)
                        for c in range(CH):
                            last = dve_v.tensor_tensor(
                                by_head(msg[:, c, :]), by_head(rows[:, c, 0:MSG]),
                                ex[:, c, :].unsqueeze(2).to_broadcast([P, H, D + 1]), ALU.mult).then_inc(msg_ready[l], 1)
                        place(n + 1, next_tile(T, k, n_T))
                        select(n + 1, FRONT)
                    if l == 0:
                        dve.wait_ge(v_ready, T + 1)
                        dve_v.tensor_scalar(neg[:, 0:C], bank[5][:, 0:C], 0.0, None, ALU.min)
                        dve_v.tensor_scalar(neg[:, C:2 * C], tp[:, C:2 * C], 0.0, None, ALU.min).then_inc(neg_ready, 1)
                    dve.wait_ge(acc_done[l], T + 1)
                    dve_v.tensor_scalar(rec[:], by_head(acc[:, 0:MSG])[:, :, D], 1e-37, None, ALU.max)
                    dve.drain()
                    dve_v.reciprocal(rec[:], rec[:])
                    dve.drain()
                    xo = xn[:, 0, :]
                    dve_v.tensor_tensor(xo.rearrange("p (h d) -> p h d", h=H), by_head(acc[:, 0:MSG])[:, :, 0:D],
                                        rec[:].unsqueeze(2).to_broadcast([P, H, D]), ALU.mult).then_inc(acc_free[l], 1)
                    dve.drain()
                    dve_v.tensor_tensor(xo, xo, b_bc[:, l, :], ALU.add)
                    dve.drain()
                    if l + 1 < LAYERS:
                        dve_v.scalar_tensor_tensor(xo, xo, LEAK, xo, ALU.mult, ALU.max).then_inc(xo_ready[l], 1)
                    else:
                        dve_v.tensor_tensor(res_tile(T), res_tile(T), xo, ALU.add)
                        dve.drain()
                    if l == 0:
                        dve.wait_ge(mix_free, T + 1)
                        dve.wait_ge(q_out, 16 * (T + 1))
                        dve.wait_ge(exp_ready, T + 1)
                        dve_v.tensor_copy(vx[:, C:C + 1], valid[:, bass.ds(T, 1)])
                        dve_v.scalar_tensor_tensor(kq[:, 0:C], bank[5][:, 0:C], 0.0, epos[:, 0:C], ALU.max, ALU.add)
                        dve_v.scalar_tensor_tensor(kq[:, C:2 * C], tp[:, C:2 * C], 0.0, epos[:, C:2 * C], ALU.max, ALU.add).then_inc(kq_ready, 1)
                    if l == 1:
                        dve.wait_ge(at_psum, T + 1)
                        dve_v.tensor_scalar(den, bank[5][:, C:2 * C], 1e-6, None, ALU.max)
                        dve.drain()
                        dve_v.reciprocal(den, den)
                        dve.drain()
                        dve_v.tensor_tensor(ats, bank[5][:, 0:C], den, ALU.mult).then_inc(ats_ready, 1)
                        dve.wait_ge(o_psum, T + 1)
                        dve_v.tensor_tensor(res_tile(T), res_tile(T), bank[6][:, 0:C], ALU.add).then_inc(o_free, 1)
                if l == 0:
                    dve.wait_ge(ctx_done, 1)
                    mask = kc[:, K_MASK:K_MASK + P]
                    for b in range(2):
                        dve_v.tensor_tensor(ctxm[:, b, :], bank[6 + b][:, b * P:(b + 1) * P], mask, ALU.mult)
                        dve_v.tensor_scalar(ksx[:, b, :], mask, bank[6 + b][:, C:C + 1], None, ALU.mult)
                    dve.drain()
                    dve.sem_inc(ctx_ready, 1)

            norm_stats(lambda i, j: res_tile(7 * i + j), mv)
            dve_v.tensor_scalar(rstd[:], mv[:, :, 1], EPS, None, ALU.add)
            dve.drain()
            dve.sem_inc(f_var, 1)
            dve.wait_ge(f_std, 1)
            dve_v.reciprocal(rstd[:], rstd[:])
            dve.drain()

            with dve.Fori(0, NT // 7) as i:
                for j in range(7):
                    T = 7 * i + j
                    dve_v.tensor_scalar(zt[:, j, :], res_tile(T), mv[:, bass.ds(T, 1), 0:1].rearrange("p a b -> p (a b)"),
                                        rstd[:, bass.ds(T, 1)], ALU.subtract, ALU.mult)
                dve.drain()
                for j in range(7):
                    dve_v.bn_stats(bst[:, j, :], zt[:, j, :])
                dve.drain()
                for j in range(7):
                    dve_v.bn_aggr(bag[:, j, :], bst[:, j, :])
                dve.drain()
                dve_v.tensor_copy(mv2[:, bass.ds(7 * i, 7), :], bag[:])
                dve.drain()
            dve_v.tensor_scalar(rstd2[:], mv2[:, :, 1], EPS, None, ALU.add).then_inc(f_var2, 1)
            dve.wait_ge(f_std2, 1)
            dve_v.reciprocal(rstd2[:], rstd2[:])
            dve.drain()

            def expert_tile(T, b, turn):
                z = xn[:, 0, :]
                dve_v.tensor_scalar(z, res_tile(T), mv[:, bass.ds(T, 1), 0:1].rearrange("p a b -> p (a b)"),
                                    rstd[:, bass.ds(T, 1)], ALU.subtract, ALU.mult)
                dve.drain()
                dve_v.tensor_scalar(z, z, mv2[:, bass.ds(T, 1), 0:1].rearrange("p a b -> p (a b)"),
                                    rstd2[:, bass.ds(T, 1)], ALU.subtract, ALU.mult).then_inc(f_xn, 1)
                lgt, mx, i8, d, t, w12, wf = (rt[:, 0:8], rt[:, 8:16], rt[:, 16:24], rt[:, 24:25], rt[:, 40:41],
                                              rt[:, 42:44], rt[:, 48:56])
                tmp = rt[:, 56:64]
                dve.wait_ge(f_lg, T + 1)
                dve_v.tensor_tensor(lgt, hp[:, 0:EXPERTS], br[:], ALU.add)
                dve.drain()
                dve_v.max(mx, lgt)
                dve.drain()
                dve_v.max_index(mi8, mx, lgt)
                dve_v.tensor_tensor(d, mx[:, 0:1], mx[:, 1:2], ALU.subtract).then_inc(f_d, 1)
                dve.drain()
                dve_v.tensor_copy(i8, mi8)
                dve.wait_ge(f_t, T + 1)
                dve_v.tensor_scalar(w12[:, 0:1], t, 0.5, 0.5, ALU.mult, ALU.add)
                dve_v.tensor_scalar(w12[:, 1:2], t, -0.5, 0.5, ALU.mult, ALU.add)
                dve.drain()
                dve_v.tensor_scalar(wf, iota[:, 0:EXPERTS], i8[:, 0:1], w12[:, 0:1], ALU.is_equal, ALU.mult)
                dve_v.tensor_scalar(tmp, iota[:, 0:EXPERTS], i8[:, 1:2], w12[:, 1:2], ALU.is_equal, ALU.mult)
                dve.drain()
                dve_v.tensor_tensor(wf, wf, tmp, ALU.add).then_inc(f_w, 1)
                dve.wait_ge(f_out[b], 16 * turn)
                dve.wait_ge(f_b2, T + 1)
                dve_v.tensor_tensor(yacc[:, b, :], res_tile(T), hp[:, 256:512], ALU.add)
                dve.drain()
                for e in range(EXPERTS):
                    dve.wait_ge(f_y, EXPERTS * T + e + 1)
                    last = dve_v.scalar_tensor_tensor(yacc[:, b, :], bank[e % 2][:, 0:C], wf[:, e:e + 1],
                                                      yacc[:, b, :], ALU.mult, ALU.add).then_inc(f_yd, 1)
                    dve.drain()
                dve.sem_inc(f_acc, 1)

            dve.sem_inc(f_yd, 2)
            expert_tile(0, 0, 1)
            with dve.Fori(0, NT // 2) as i:
                expert_tile(2 * i + 1, 1, i + 1)
                expert_tile(2 * i + 2, 0, i + 2)

        @block.tensor
        def _(pe):
            pe.wait_ge(k_in, 16)
            pe.wait_ge(flags_ready, 1)
            fl = small[:, 128:128 + 2 * NT].rearrange("p (w t) -> p w t", w=2)
            pe.matmul(tp[0:NT, 0:P], fl[:, 0, :], ident, start=True, stop=True)
            pe.matmul(tp[0:NT, P:2 * P], fl[:, 1, :], ident, start=True, stop=True).then_inc(flagsT_ready, 1)
            pe.wait_ge(slots_ready, 1)
            n_f = small[0:NT, 243:244]
            pe.matmul(tp[0:NT, 256:257], kc[0:NT, K_TRI:K_TRI + NT], n_f, start=True, stop=True)
            pe.matmul(tp[0:NT, 257:258], ones[0:NT, 0:NT], n_f, start=True, stop=True).then_inc(sums_ready, 1)
            pe.wait_ge(ctl_ready, 1)
            pe.wait_ge(ext_ready, 1)
            pe.wait_ge(zeros_ready, 2)
            pe.sem_inc(xn_free, 2)

            def project(T, l, b, s_before=None):
                pe.wait_ge(hp_free[l], T + 1)
                for k in range(2):
                    last = pe.matmul(hp[:, 0:EXT], xT[:, b, k, :], wext[:, l, k, :], start=(k == 0), stop=(k == 1))
                    if k == 0 and s_before is not None:
                        last.then_inc(s_before, 1)
                last.then_inc(h_done[l], 1)

            def turn_tile(src, s_done):
                pe.transpose(tp[:, 0:P], src[:, 0:P], ident)
                pe.transpose(tp[:, P:2 * P], src[:, P:C], ident).then_inc(s_done, 1)

            def first(T, b):
                pe.wait_ge(xT_ready, T + 1)
                pe.wait_ge(xn_ready, T + 2)
                turn_tile(xn[:, 1 - b, :], xT_psum)
                project(T, 0, b, xn_free)

            pe.wait_ge(xn_ready, 1)
            turn_tile(xn[:, 0, :], xT_psum)
            with pe.Fori(0, NT // 2) as i:
                first(2 * i, 0)
                first(2 * i + 1, 1)
            pe.wait_ge(xT_ready, NT)
            project(NT - 1, 0, 0)

            def zeros(dst, start, stop):
                return pe.matmul(dst, zb[:, 0:P], zb[:, 0:dst.shape[1]], start=start, stop=stop)

            for l in range(LAYERS):
                pe.wait_ge(extremes[l], 1)
                pe.matmul(tp[0:2 * H, 0:P], small[:, 0:2 * H], ident, start=True, stop=True).then_inc(extremesT[l], 1)
                pe.wait_ge(spread[l], 1)
                pe.matmul(tp[:, 0:2 * H], ones[0:2 * H, :], small[0:2 * H, 32:48], start=True, stop=True).then_inc(spread_done[l], 1)

                def prepare(n, T):
                    pe.wait_ge(selT_ready[l], n + 1)
                    for c in range(CH):
                        for part in range(3):
                            last = pe.matmul(uv_p[:, c * UV:(c + 1) * UV], selT[:, c, :],
                                             uvb[:, part, bass.ds(T, 1), :].rearrange("p a b -> p (a b)"),
                                             start=(part == 0), stop=(part == 2))
                    last.then_inc(uv_ready[l], 1)

                pe.wait_ge(uvb_ready[l], 1)
                if l == 0:
                    pe.wait_ge(late_in, 16 * LATE)
                    pe.sem_inc(mix_free, 1)
                    for b in range(2):
                        zeros(bank[6 + b][:, 0:C + 1], True, False)
                prepare(0, 0)
                with pe.Fori(0, NT) as T:
                    n_T, before = tile_ctl(pe, T)
                    pe.wait_ge(acc_free[l], T + 1)
                    zeros(acc[:, 0:MSG], True, False)
                    with pe.Fori(0, n_T) as k:
                        n = before + k
                        prepare(n + 1, next_tile(T, k, n_T))
                        for c in range(CH):
                            pe.wait_ge(sel_ready[l], CH * n + c + 1)
                            pe.wait_ge(msg_ready[l], CH * n + c + 1)
                            pe.matmul(acc[:, 0:MSG], sel[:, c, :], msg[:, c, :], start=False, stop=False).then_inc(agg_done[l], 1)
                    zeros(acc[:, 0:MSG], False, True).then_inc(acc_done[l], 1)
                    if l == 0:
                        pe.wait_ge(xnT_in, 16 * (T + 1))
                        for c in range(2):
                            pe.matmul(bank[5][:, :], xnTs[:, c, :], wkvT[:, c, :], start=(c == 0), stop=(c == 1))
                        for o in range(2):
                            for c in range(2):
                                last = pe.matmul(tp[:, C + o * P:C + (o + 1) * P], wqT[:, c, o * P:(o + 1) * P], xnTs[:, c, :],
                                                 start=(c == 0), stop=(c == 1))
                        last.then_inc(mix_psum, 1)
                    if l == 1:
                        pe.wait_ge(ctx_ready, 1)
                        pe.wait_ge(qT_in, 16 * (T + 1))
                        for b in range(2):
                            pe.matmul(bank[5][:, b * P:(b + 1) * P], ctxm[:, b, :], qTs[:, b, :], start=True, stop=True)
                            last = pe.matmul(bank[5][:, C + b * P:C + (b + 1) * P], ksx[:, b, :], qTs[:, b, :], start=True, stop=True)
                        last.then_inc(at_psum, 1)
                    if l == 0:
                        pe.wait_ge(kq_ready, T + 1)
                        pe.wait_ge(v_ready, T + 1)
                        for b in range(2):
                            last = pe.matmul(bank[6 + b][:, 0:C + 1], kq[:, b * P:(b + 1) * P], vx, start=False, stop=False)
                        last.then_inc(mix_free, 1)
                    if l + 1 < LAYERS:
                        pe.wait_ge(xo_ready[l], T + 1)
                        turn_tile(xn[:, 0, :], xoT_psum[l])
                        pe.wait_ge(xoT_ready[l], T + 1)
                        project(T, l + 1, 0)
                    if l == 1:
                        pe.wait_ge(ats_ready, T + 1)
                        pe.wait_ge(o_free, T + 1)
                        for b in range(2):
                            last = pe.matmul(bank[6][:, 0:C], ats[:, b * P:(b + 1) * P], wpT[:, b, :], start=(b == 0), stop=(b == 1))
                        last.then_inc(o_psum, 1)
                if l == 0:
                    zeros(bank[6][:, 0:C + 1], False, True)
                    zeros(bank[7][:, 0:C + 1], False, True).then_inc(ctx_done, 1)

            with pe.Fori(0, NT) as T:
                pe.wait_ge(f_xn, T + 1)
                turn_tile(xn[:, 0, :], f_tp)
                pe.wait_ge(f_xT, 2 * (T + 1))
                for c in range(2):
                    last = pe.matmul(hp[:, 0:EXPERTS], xT[:, 0, c, :], wr[:, c, :], start=(c == 0), stop=(c == 1))
                last.then_inc(f_lg, 1)

                def up(e):
                    for k in range(HB):
                        for c in range(2):
                            last = pe.matmul(bank[5 + e % 2][:, k * P:(k + 1) * P], w1[:, e, c, k * P:(k + 1) * P],
                                             xT[:, 0, c, :], start=(c == 0), stop=(c == 1))
                    last.then_inc(f_h, 1)

                def down(e):
                    pe.wait_ge(f_g, EXPERTS * T + e + 1)
                    pe.wait_ge(f_yd, EXPERTS * T + e + 1)
                    for k in range(HB):
                        last = pe.matmul(bank[e % 2][:, 0:C], gT[:, e % 2, k, :], w2[:, e, k, :],
                                         start=(k == 0), stop=(k == HB - 1))
                    last.then_inc(f_y, 1)

                up(0)
                up(1)
                pe.wait_ge(f_w, T + 1)
                pe.matmul(hp[0:EXPERTS, P:2 * P], rt[:, 48:48 + EXPERTS], ident, start=True, stop=True).then_inc(f_wT_p, 1)
                down(0)
                pe.wait_ge(f_wT, T + 1)
                pe.matmul(hp[:, C:2 * C], wT, b2[:], start=True, stop=True).then_inc(f_b2, 1)
                for e in range(2, EXPERTS):
                    up(e)
                    down(e - 1)
                down(EXPERTS - 1)


def kernel(**inputs):
    import concourse.bacc as bacc
    from concourse.bass_utils import run_bass_kernel_spmd

    v = {n: np.asarray(x) for n, x in inputs.items()}
    edges = np.zeros((EP, 2), np.int32)
    edges[:, 1] = NO_NODE
    edges[:E, 0] = v["src"]
    edges[:E, 1] = v["dst"]
    x = np.zeros((NP, C), np.float32)
    x[:N] = v["x"]
    named = {
        "x": x, "edges": edges.reshape(-1), "dst": np.ascontiguousarray(edges[:, 1]), "consts": constants(),
        "W": v["L0_gnn_W"], "al": v["L0_gnn_al"].reshape(LAYERS, C), "ar": v["L0_gnn_ar"].reshape(LAYERS, C),
        "b": v["L0_gnn_b"], "wqT": v["L0_mix_Wq"].T, "wkvT": v["L0_mix_Wkv"].T, "wpT": v["L0_mix_Wproj"].T,
        "bproj": v["L0_mix_bproj"], "br": v["L0_ffn_br"], "Wr": v["L0_ffn_Wr"], "W1": v["L0_ffn_W1"],
        "b1": v["L0_ffn_b1"].reshape(EXPERTS * HB, P).T, "W2": v["L0_ffn_W2"], "b2": v["L0_ffn_b2"],
        "gb": np.concatenate([v["L0_ffn_gamma"].reshape(2, P), v["L0_ffn_beta"].reshape(2, P)]).T,
    }
    nc = bacc.Bacc("TRN2", target_bir_lowering=False, num_devices=1)
    arrays, aps = {}, {}
    for name, array in named.items():
        arrays[f"in_{name}"] = np.ascontiguousarray(array)
        aps[name] = nc.dram_tensor(f"in_{name}", array.shape, mybir.dt.from_np(array.dtype), kind="ExternalInput").ap()
    out = nc.dram_tensor("out_x", (NP, C), F32, kind="ExternalOutput").ap()
    build(nc, aps, out)
    nc.compile()
    r = run_bass_kernel_spmd(nc, [arrays], core_ids=[0])
    return r.results[0]["out_x"][:N]
```

```python
import numpy as np
import concourse.bass as bass
from concourse import mybir
from contextlib import ExitStack

F32 = mybir.dt.float32
BF16 = mybir.dt.bfloat16
I32 = mybir.dt.int32
U32 = mybir.dt.uint32
ALU = mybir.AluOpType
ACT = mybir.ActivationFunctionType
AX = mybir.AxisListType

P = 128
N = 6250
E = 200000
C = 256
H = 8
D = C // H
LAYERS = 3
NT = -(-N // P)
NP = NT * P
CH = 4
SLOT = CH * P
RING = 4
CELL = 64
CELLS = -(-E // (CELL * P))
EP = CELLS * CELL * P
NO_NODE = 65536
BIG = 4096
EXT = C + 3 * H
MSG = H * (D + 1)
ROW = MSG + 2 * H
UV = 2 * H
EXPERTS = 8
HID = 512
HB = HID // P
SLOPE = 0.2
LEAK = 0.01
EPS = 1e-5
R_LOGIT, R_MAX, R_INDEX, R_D, R_T, R_W12, R_W = 0, 8, 16, 24, 28, 32, 40
SAFE = 60.0
LOW = -1e30

K_ID, K_IOTA, K_BASE, K_VALID, K_CELL, K_CINV, K_TRI, K_LAST, K_MASK, K_ONE, K_NODE = (
    0, P, 2 * P, 2 * P + NT + 1, 2 * P + 2 * NT + 1, 2 * P + 2 * NT + 1 + CELLS, 2 * P + 2 * NT + 1 + 2 * CELLS,
    2 * P + 3 * NT + 1 + 2 * CELLS, 2 * P + 3 * NT + 2 + 2 * CELLS, 3 * P + 3 * NT + 2 + 2 * CELLS,
    4 * P + 3 * NT + 2 + 2 * CELLS)
K_ALL = K_NODE + NT + 1


def constants():
    k = np.zeros((P, K_ALL), np.float32)
    p = np.arange(P)[:, None]
    k[:, K_ID:K_IOTA] = np.eye(P)
    k[:, K_IOTA:K_BASE] = np.arange(P)
    k[:, K_BASE:K_VALID] = P * np.arange(NT + 1)
    k[:, K_VALID:K_CELL] = p + P * np.arange(NT) < N
    cell = p * CELLS + np.arange(CELLS)
    k[:, K_CELL:K_CINV] = cell + 1
    k[:, K_CINV:K_TRI] = BIG - cell
    k[:, K_TRI:K_LAST] = p < np.arange(NT)
    k[:, K_LAST] = np.arange(P) == NT - 1
    k[:, K_MASK:K_ONE] = p // D == np.arange(P) // D
    k[:, K_ONE:K_NODE] = 1
    k[:, K_NODE:] = p + P * np.arange(NT + 1)
    return k


def build(nc, a, out):
    es = ExitStack()
    with es:
        def sb(name, shape, dt=F32):
            return es.enter_context(nc.sbuf_tensor(name, shape, dt))

        def sem(name):
            return es.enter_context(nc.semaphore(name))

        table = [nc.dram_tensor(f"table{l}", (NP, ROW), F32).ap() for l in range(LAYERS)]
        xnT_d = nc.dram_tensor("xnT_d", (NT, P, C), F32).ap()
        qT_d = nc.dram_tensor("qT_d", (NT, P, C), F32).ap()
        ctl_d = nc.dram_tensor("ctl_d", (NT, 4), I32).ap()

        kc = sb("kc", [P, K_ALL])
        ident, iota = kc[:, K_ID:K_IOTA], kc[:, K_IOTA:K_BASE]
        ones = kc[:, K_ONE:K_ONE + P]
        node = kc[:, K_NODE:K_ALL]
        base, valid = kc[:, K_BASE:K_VALID], kc[:, K_VALID:K_CELL]
        res = sb("res", [P, NT, C])
        wext = sb("wext", [P, LAYERS, 2, EXT])
        b_bc = sb("b_bc", [P, LAYERS, C])
        bproj = sb("bproj", [P, C])
        wqT = sb("wqT", [P, 2, C])
        wkvT = sb("wkvT", [P, 2, 2 * C])
        wpT = sb("wpT", [P, 2, C])
        w1 = sb("w1", [P, EXPERTS, 2, HID])
        w2 = sb("w2", [P, EXPERTS, HB, C])
        b1 = sb("b1", [P, EXPERTS * HB])
        b2 = sb("b2", [EXPERTS, C])
        wr = sb("wr", [P, 2, EXPERTS])
        gb = sb("gb", [P, 4])
        br = sb("br", [P, EXPERTS])
        eler = sb("eler", [P, NT, 3 * H])
        uv = sb("uv", [P, NT, UV])
        uvb = sb("uvb", [P, 3, NT + 1, UV], BF16)
        meta = sb("meta", [P, RING, CH, 2], I32)
        dstb = sb("dstb", [P, RING, SLOT], I32)
        gat = sb("gat", [P, RING, CH, ROW])
        dl = sb("dl", [P, CH])
        sel = sb("sel", [P, CH, P])
        selT = sb("selT", [P, CH, P], BF16)
        lg2 = sb("lg2", [P, CH, UV])
        lg = sb("lg", [P, CH, H])
        ex = sb("ex", [P, CH, H])
        msg = sb("msg", [P, CH, MSG])
        zb = sb("zb", [P, MSG], BF16)
        ctl = sb("ctl", [1, NT, 4], I32)
        small = sb("small", [P, 512])
        ismall = sb("ismall", [P, 64], I32)
        mv = sb("mv", [P, NT, 2])
        bst = sb("bst", [P, 7, 6])
        bag = sb("bag", [P, 7, 2])
        rstd = sb("rstd", [P, NT])
        deviate = sb("deviate", [P, 1])[:]
        warm = sb("warm", [P, 2])
        xn = sb("xn", [P, 2, C])
        xT = sb("xT", [P, 2, 2, P])
        hrow = sb("hrow", [P, 2, ROW])
        rec = sb("rec", [P, H])
        region = sb("region", [P, 3456])
        dcell = region[:, 0:CELLS * CELL].bitcast(I32).rearrange("p (a b) -> p a b", b=CELL)
        albc = region[:, 1600:1600 + LAYERS * C].rearrange("p (l c) -> p l c", c=C)
        arbc = region[:, 2400:2400 + LAYERS * C].rearrange("p (l c) -> p l c", c=C)
        hit = gat[:, :, :, :].rearrange("p a b c -> p (a b c)")
        xnTs = region[:, 0:256].rearrange("p (b n) -> p b n", b=2)
        span_flag = ismall[0:1, 8:9]
        seg = msg[:, :, :].rearrange("p c m -> p (c m)")[:, 0:H * P].rearrange("p (h n) -> p h n", h=H)
        neg = region[:, 256:768]
        epos = region[:, 768:1280]
        kq = region[:, 1280:1792]
        vx = region[:, 1792:1792 + C + 1]
        ctxm = region[:, 2060:2316].rearrange("p (b n) -> p b n", b=2)
        ksx = region[:, 2316:2572].rearrange("p (b n) -> p b n", b=2)
        qTs = region[:, 2572:2828].rearrange("p (b n) -> p b n", b=2)
        den = region[:, 2828:3084]
        ats = region[:, 3084:3340]
        gT = region[:, 0:1024].rearrange("p (s b n) -> p s b n", s=2, b=HB)
        yacc = region[:, 1024:1536].rearrange("p (s c) -> p s c", s=2)
        rt = region[:, 1536:1664].rearrange("p (s c) -> p s c", s=2)
        wT = region[0:EXPERTS, 1700:1828]
        mi8 = region[:, 1830:1838].bitcast(U32)

        def by_head(x):
            return x.rearrange("p (h d) -> p h d", h=H)

        bank = [es.enter_context(nc.psum_tensor(f"bank{i}", [P, 512], F32)) for i in range(8)]
        acc = bank[0]
        uv_p = bank[2]
        y_psum = (bank[1], bank[7])
        q_psum = bank[1][:, 0:C]
        tp = bank[3]
        hp = bank[4]
        first_tp, first_hp = (tp, bank[2]), (hp, bank[5])

        x_in, k_in, w_in, d_in, late_in = map(sem, ("x_in", "k_in", "w_in", "d_in", "late_in"))
        ext_ready, var_ready, std_ready, flags_ready, flagsT_ready, slots_ready, sums_ready, ctl_ready = map(
            sem, ("ext_ready", "var_ready", "std_ready", "flags_ready", "flagsT_ready", "slots_ready", "sums_ready",
                  "ctl_ready"))
        ctl_out, ctl_in, zeros_ready = sem("ctl_out"), sem("ctl_in"), sem("zeros_ready")
        xn_ready, xn_free, xT_psum, xT_ready = map(sem, ("xn_ready", "xn_free", "xT_psum", "xT_ready"))
        xT_out = [sem("xT_out0"), sem("xT_out1")]
        h_done, hp_free = ([sem(f"{n}{l}") for l in range(LAYERS)] for n in ("h_done", "hp_free"))
        row_out = [[sem(f"row_out{l}_{b}") for b in range(2)] for l in range(LAYERS)]
        (meta_in, dst_in, meta_ready, gathered, slot_free, dl_read, selT_ready, uv_ready, logit_ready, ex_ready,
         msg_ready, agg_done, acc_done, acc_free) = (
            [sem(f"{n}{l}") for l in range(LAYERS)] for n in (
                "meta_in", "dst_in", "meta_ready", "gathered", "slot_free",
                "dl_read", "selT_ready", "uv_ready", "logit_ready", "ex_ready", "msg_ready",
                "agg_done", "acc_done", "acc_free"))
        xo_ready, xoT_psum, xoT_ready = (
            [sem(f"{n}{l}") for l in range(LAYERS - 1)] for n in ("xo_ready", "xoT_psum", "xoT_ready"))
        seg_free, seg_meta, seg_rows, seg_max, seg_turned = (
            [sem(f"{n}{l}") for l in range(LAYERS)] for n in ("seg_free", "seg_meta", "seg_rows", "seg_max", "seg_turned"))
        extremes, extremesT, spread, spread_done, span_ready, uvb_ready, slot_taken, seg_taken = map(
            sem, ("extremes", "extremesT", "spread", "spread_done", "span_ready", "uvb_ready", "slot_taken", "seg_taken"))
        slot_in = [[sem(f"slot_in{l}_{r}") for r in range(RING)] for l in range(LAYERS)]
        xnT_in, mix_psum, neg_ready, exp_ready, v_ready, kq_ready, mix_free, q_out, ctx_done, ctx_ready = map(
            sem, ("xnT_in", "mix_psum", "neg_ready", "exp_ready", "v_ready", "kq_ready", "mix_free", "q_out",
                  "ctx_done", "ctx_ready"))
        qT_in, at_psum, ats_ready, o_psum, o_free = map(sem, ("qT_in", "at_psum", "ats_ready", "o_psum", "o_free"))
        f_var, f_std = sem("f_var"), sem("f_std")
        f_xn, f_tp, f_xT, f_lg, f_d, f_t, f_w, f_wT_p, f_wT, f_b2, f_h, f_g, f_y, f_yd, f_acc = map(
            sem, ("f_xn", "f_tp", "f_xT", "f_lg", "f_d", "f_t", "f_w", "f_wT_p", "f_wT", "f_b2", "f_h", "f_g",
                  "f_y", "f_yd", "f_acc"))
        f_out = [sem("f_out0"), sem("f_out1")]
        ROWS = [[16 * (NT // 2 + 2), 16 * (NT // 2 + 1)]] + [[16 * (NT + 1), 0]] * (LAYERS - 1)
        LATE = 12
        FRONT, BACK = range(0, CH // 2), range(CH // 2, CH)

        block = es.enter_context(nc.Block())


        def tile_ctl(eng, T):
            n = eng.value_load(ctl[0:1, bass.ds(T, 1), 1:2].rearrange("a b c -> a (b c)"), min_val=1, max_val=SLOTS_MAX)
            before = eng.value_load(ctl[0:1, bass.ds(T, 1), 2:3].rearrange("a b c -> a (b c)"), min_val=0, max_val=TOTAL_MAX)
            return n, before

        def exact_asked(eng, l):
            eng.wait_ge(ctl_in, 16)
            eng.wait_ge(span_ready, l + 1)
            return eng.value_load(span_flag, min_val=0, max_val=1)

        def next_tile(T, k, n):
            return nc.s_assert_within(T + (k + 1) // n, 0, NT, skip_runtime_bounds_check_because="k < n")

        SLOTS_MAX = EP // SLOT + RING
        TOTAL_MAX = NT * SLOTS_MAX

        @block.sync
        def _(sp):
            sp.dma_start(dcell, a["dst"].rearrange("(p a b) -> p a b", p=P, b=CELL)).then_inc(d_in, 16)
            sp.dma_start(kc[:], a["consts"]).then_inc(k_in, 16)
            sp.dma_start(res[:], a["x"].rearrange("(t p) c -> p t c", p=P)).then_inc(x_in, 16)
            for l in range(LAYERS):
                sp.dma_start(wext[:, l, :, 0:C], a["W"][l].rearrange("(k p) c -> p k c", p=P)).then_inc(w_in, 16)
            sp.dma_start(albc, a["al"].rearrange("(a l) c -> a l c", a=1).to_broadcast([P, LAYERS, C])).then_inc(w_in, 16)
            sp.dma_start(arbc, a["ar"].rearrange("(a l) c -> a l c", a=1).to_broadcast([P, LAYERS, C])).then_inc(w_in, 16)
            for dst, src in ((b_bc[:], a["b"].rearrange("(a l) c -> a l c", a=1).to_broadcast([P, LAYERS, C])),
                             (bproj[:], a["bproj"].rearrange("(a c) -> a c", a=1).to_broadcast([P, C])),
                             (br[:], a["br"].rearrange("(a c) -> a c", a=1).to_broadcast([P, EXPERTS])),
                             (wqT[:], a["wqT"].rearrange("(k p) c -> p k c", p=P)),
                             (wkvT[:], a["wkvT"].rearrange("(k p) c -> p k c", p=P)),
                             (wpT[:], a["wpT"].rearrange("(k p) c -> p k c", p=P)),
                             (w1[:, :, :, :], a["W1"].rearrange("e (k p) h -> p e k h", p=P)),
                             (w2[:, :, :, :], a["W2"].rearrange("e (k p) c -> p e k c", p=P)),
                             (b1[:], a["b1"]), (b2[:], a["b2"]), (gb[:], a["gb"]),
                             (wr[:], a["Wr"].rearrange("(k p) c -> p k c", p=P))):
                sp.dma_start(dst, src).then_inc(late_in, 16)
            sp.wait_ge(ctl_ready, 1)
            sp.dma_start(ctl_d, ismall[0:NT, 4:8]).then_inc(ctl_out, 16)
            sp.wait_ge(ctl_out, 16)
            sp.dma_start(ctl[:], ctl_d.rearrange("(a t) c -> a t c", a=1)).then_inc(ctl_in, 16)

            def first_store(T, b):
                sp.wait_ge(xT_ready, T + 1)
                sp.dma_start(xnT_d[bass.ds(T, 1), :, :].rearrange("a p c -> (a p) c"),
                             xT[:, b, :, :].rearrange("p a b -> p (a b)")).then_inc(xT_out[b], 16)
                sp.wait_ge(hp_free[0], T + 3)
                sp.dma_start(table[0][bass.ds(T * P, P), :], hrow[:, b, :]).then_inc(row_out[0][b], 16)

            first_store(0, 0)
            with sp.Fori(0, NT // 2) as i:
                first_store(2 * i + 1, 1)
                first_store(2 * i + 2, 0)
            sp.wait_ge(ctl_in, 16)

            for l in range(LAYERS):
                def load_slot(edge, n):
                    sp.wait_ge(slot_free[l], n + 1)
                    sp.sem_inc(slot_taken, 1)
                    sp.dma_start(meta[:, bass.ds(n % RING, 1), :, :].rearrange("p a c w -> p (a c w)"),
                                 a["edges"][bass.ds(2 * edge, SLOT * 2)].rearrange("(p f) -> p f", p=P)).then_inc(meta_in[l], 16)
                    sp.dma_start(dstb[:, bass.ds(n % RING, 1), :].rearrange("p a e -> p (a e)"),
                                 a["dst"][bass.ds(edge, SLOT)].rearrange("(a e) -> a e", a=1).to_broadcast([P, SLOT])
                                 ).then_inc(dst_in[l], 16)
                    sp.wait_ge(meta_in[l], 16 * (n + 1))
                    sp.wait_ge(dst_in[l], 16 * (n + 1))
                    sp.sem_inc(meta_ready[l], 1)

                with sp.If(exact_asked(sp, l) > 0), sp.Fori(0, NT) as T:
                    n_T, before = tile_ctl(sp, T)
                    start = sp.value_load(ctl[0:1, bass.ds(T, 1), 0:1].rearrange("a b c -> a (b c)"), min_val=0, max_val=EP)
                    with sp.Fori(0, n_T) as k:
                        edge = nc.s_assert_within(start + k * SLOT, 0, EP - SLOT,
                                                  skip_runtime_bounds_check_because="a tile's slots end inside the padding")
                        sp.wait_ge(seg_free[l], before + k + 1)
                        sp.sem_inc(seg_taken, 1)
                        sp.dma_start(meta[:, 0, :, :].rearrange("p c w -> p (c w)"),
                                     a["edges"][bass.ds(2 * edge, SLOT * 2)].rearrange("(p f) -> p f", p=P)).then_inc(seg_meta[l], 16)

                with sp.Fori(0, NT) as T:
                    n_T, before = tile_ctl(sp, T)
                    start = sp.value_load(ctl[0:1, bass.ds(T, 1), 0:1].rearrange("a b c -> a (b c)"), min_val=0, max_val=EP)
                    with sp.Fori(0, n_T) as k:
                        edge = nc.s_assert_within(start + k * SLOT, 0, EP - SLOT,
                                                  skip_runtime_bounds_check_because="a tile's slots end inside the padding")
                        load_slot(edge, before + k)
                rounds = sp.value_load(ctl[0:1, 0:1, 3:4].rearrange("a b c -> a (b c)"), min_val=12, max_val=TOTAL_MAX // RING)
                load_slot(0, rounds * RING + RING)

            for b in range(2):
                sp.wait_ge(f_out[b], ROWS[0][b])

        @block.gpsimd
        def _(pool):
            pool.memset(zb[:], 0.0).then_inc(zeros_ready, 1)
            pool.memset(hrow[:], 1.0).then_inc(zeros_ready, 1)
            pool.wait_ge(ctl_in, 16)
            rounds = pool.value_load(ctl[0:1, 0:1, 3:4].rearrange("a b c -> a (b c)"), min_val=12, max_val=TOTAL_MAX // RING)
            for l in range(LAYERS):
                def gather_rows(r, s_done):
                    for c in range(CH):
                        pool.indirect_dma_start(gat[:, r, c, :], None, table[l],
                                                bass.IndirectOffsetOnAxis(meta[:, r, c, 0:1].bitcast(U32), 0)
                                                ).then_inc(s_done, 16)

                def ready(n):
                    pool.wait_ge(slot_free[l], n + 1)
                    pool.wait_ge(meta_ready[l], n + 1)

                def announce(r, turn):
                    pool.wait_ge(slot_in[l][r], 16 * CH * turn)
                    pool.sem_inc(gathered[l], 1)

                for b in range(2):
                    if ROWS[l][b]:
                        pool.wait_ge(row_out[l][b], ROWS[l][b])
                with pool.If(exact_asked(pool, l) > 0), pool.Fori(0, NT) as T:
                    n_T, before = tile_ctl(pool, T)
                    with pool.Fori(0, n_T) as k:
                        pool.wait_ge(seg_meta[l], 16 * (before + k + 1))
                        pool.sem_inc(seg_taken, 1)
                        gather_rows(0, seg_rows[l])
                for n in range(2):
                    ready(n)
                    gather_rows(n, slot_in[l][n])
                with pool.Fori(0, rounds) as i:
                    for j in range(RING):
                        n = RING * i + 2 + j
                        ready(n)
                        announce(j, i + 1)
                        gather_rows((2 + j) % RING, slot_in[l][(2 + j) % RING])
                for j in range(2):
                    ready(RING * rounds + 2 + j)
                    announce(j, rounds + 1)
                    gather_rows(2 + j, slot_in[l][2 + j])
                for j in range(2, RING):
                    announce(j, rounds + 1)

        @block.scalar
        def _(act):
            def row_copy(T, b, l, turn, psum):
                act.wait_ge(row_out[l][b], 16 * turn)
                act.wait_ge(h_done[l], T + 1)
                act.activation(by_head(hrow[:, b, 0:MSG])[:, :, 0:D], psum[:, 0:C].rearrange("p (h d) -> p h d", h=H), ACT.Copy)
                act.activation(hrow[:, b, MSG:ROW], psum[:, C:C + UV], ACT.Copy)
                act.activation(eler[:, bass.ds(T, 1), :].rearrange("p a c -> p (a c)"), psum[:, C:EXT], ACT.Copy).then_inc(hp_free[l], 1)

            for b in range(2):
                act.sem_inc(row_out[0][b], 16)
                act.sem_inc(xT_out[b], 16)
            act.sem_inc(hp_free[0], 2)
            act.wait_ge(zeros_ready, 2)
            act.wait_ge(var_ready, 1)
            act.activation(rstd[:], rstd[:], ACT.Sqrt).then_inc(std_ready, 1)

            def first_copy(T, b, turn):
                act.wait_ge(xT_out[b], 16 * turn)
                act.wait_ge(xT_psum, T + 1)
                act.activation(xT[:, b, :, :].rearrange("p a b -> p (a b)"), first_tp[b][:, 0:C], ACT.Copy).then_inc(xT_ready, 1)

            first_copy(0, 0, 1)
            with act.Fori(0, NT // 2) as i:
                first_copy(2 * i + 1, 1, i + 1)
                row_copy(2 * i, 0, 0, i + 1, first_hp[0])
                first_copy(2 * i + 2, 0, i + 2)
                row_copy(2 * i + 1, 1, 0, i + 1, first_hp[1])
            row_copy(NT - 1, 0, 0, NT // 2 + 1, first_hp[0])
            for b in range(2):
                act.wait_ge(xT_out[b], ROWS[0][b])

            def deviation(T):
                act.wait_ge(f_var, T + 1)
                act.activation(deviate, deviate, ACT.Sqrt).then_inc(f_std, 1)

            def gelu(T, e):
                act.wait_ge(f_h, EXPERTS * T + e + 1)
                for k in range(HB):
                    last = act.activation(gT[:, e % 2, k, :], bank[5 + e % 2][:, k * P:(k + 1) * P], ACT.Gelu,
                                          bias=b1[:, e * HB + k:e * HB + k + 1])
                last.then_inc(f_g, 1)

            def to_features(T, b):
                act.wait_ge(f_tp, T + 1)
                for c in range(2):
                    act.activation(xT[:, b, c, :], tp[:, c * P:(c + 1) * P], ACT.Identity,
                                   bias=gb[:, 2 + c:3 + c], scale=gb[:, c:c + 1]).then_inc(f_xT, 1)

            def router_tanh(T, b):
                act.wait_ge(f_d, T + 1)
                act.activation(rt[:, b, R_T:R_T + 1], rt[:, b, R_D:R_D + 1], ACT.Tanh, scale=0.5).then_inc(f_t, 1)

            def weights_copy(T):
                act.wait_ge(f_wT_p, T + 1)
                act.activation(wT, hp[0:EXPERTS, P:2 * P], ACT.Copy).then_inc(f_wT, 1)

            def expert_tile(T, b, following):
                for e in range(EXPERTS):
                    gelu(T, e)
                    if following and e == 0:
                        deviation(T + 1)
                    if following and e == 2:
                        to_features(T + 1, 1 - b)
                    if following and e == 5:
                        router_tanh(T + 1, 1 - b)
                    if following and e == 6:
                        weights_copy(T + 1)
                act.wait_ge(f_acc, T + 1)
                act.dma_start(out[bass.ds(T * P, P), :], yacc[:, b, :]).then_inc(f_out[b], 16)

            for l in range(LAYERS):
                if l + 1 < LAYERS:
                    act.sem_inc(row_out[l + 1][0], 16)
                    act.sem_inc(hp_free[l + 1], 1)
                if l == 0:
                    act.sem_inc(q_out, 16)

                act.wait_ge(ctl_in, 16)
                def tile(T):
                    n_T, before = tile_ctl(act, T)
                    if l + 1 == LAYERS:
                        act.activation(warm[:, 1:2], warm[:, 0:1], ACT.Exp)
                    with act.Fori(0, n_T) as k:
                        n = before + k
                        act.wait_ge(logit_ready[l], n + 1)
                        act.activation(ex[:], lg[:], ACT.Relu, scale=-1.0)
                        act.drain()
                        act.activation(ex[:], ex[:], ACT.Exp, scale=-1.0).then_inc(ex_ready[l], 1)
                    following = 0 if l + 1 == LAYERS else (T + 1) % NT
                    if l == 0:
                        act.wait_ge(mix_psum, T + 1)
                        act.wait_ge(mix_free, T + 1)
                        act.activation(vx[:, 0:C], bank[5][:, C:2 * C], ACT.Copy).then_inc(v_ready, 1)
                        load_input(following)
                    if l == 1:
                        act.wait_ge(at_psum, T + 1)
                        load_queries(following)
                    if l == 0:
                        act.wait_ge(neg_ready, T + 1)
                        act.activation(epos, neg, ACT.Exp).then_inc(exp_ready, 1)
                    if l + 1 < LAYERS:
                        act.wait_ge(xoT_psum[l], T + 1)
                        act.activation(xT[:, 0, :, :].rearrange("p a b -> p (a b)"), tp[:, 0:C], ACT.Copy).then_inc(xoT_ready[l], 1)
                        row_copy(T, 0, l + 1, T + 1, hp)
                        act.drain()
                        act.dma_start(table[l + 1][bass.ds(T * P, P), :], hrow[:, 0, :]).then_inc(row_out[l + 1][0], 16)
                    if l == 0:
                        act.wait_ge(kq_ready, T + 1)
                        act.dma_start(qT_d[bass.ds(T, 1), :, :].rearrange("a p c -> (a p) c"), kq[:, C:2 * C]).then_inc(q_out, 16)
                def load_input(T):
                    act.dma_start(xnTs.rearrange("p b n -> p (b n)"),
                                  xnT_d[bass.ds(T, 1), :, :].rearrange("a p c -> (a p) c")).then_inc(xnT_in, 16)

                def load_queries(T):
                    act.dma_start(qTs.rearrange("p b n -> p (b n)"),
                                  qT_d[bass.ds(T, 1), :, :].rearrange("a p c -> (a p) c")).then_inc(qT_in, 16)

                if l == 0:
                    act.activation(warm[:, 0:1], zb[:, 0:1], ACT.Copy)
                    act.drain()
                    act.activation(warm[:, 1:2], warm[:, 0:1], ACT.Exp)
                    load_input(0)
                if l == 1:
                    load_queries(0)
                if l + 1 < LAYERS:
                    with act.Fori(0, NT) as T:
                        tile(T)
                    act.wait_ge(xnT_in if l == 0 else qT_in, 16 * (NT + 1))
                else:
                    act.wait_ge(late_in, 16 * LATE)
                    for b in range(2):
                        act.sem_inc(f_out[b], 16)
                    tile(0)
                    deviation(0)
                    to_features(0, 0)
                    router_tanh(0, 0)
                    weights_copy(0)
                    with act.Fori(0, NT // 2) as i:
                        tile(2 * i + 1)
                        expert_tile(2 * i, 0, True)
                        tile(2 * i + 2)
                        expert_tile(2 * i + 1, 1, True)
                    expert_tile(NT - 1, 0, False)
                if l == 0:
                    act.wait_ge(q_out, 16 * (NT + 1))

        @block.vector
        def _(dve):
            dve_v = nc.vector

            dve.wait_ge(w_in, 16 * (LAYERS + 2))
            hv = hit[:, 0:LAYERS * 2 * C].rearrange("p (l k c) -> p l k c", l=LAYERS, k=2)
            hr = hit[:, 0:LAYERS * 2 * C].rearrange("p (l h d) -> p l h d", l=LAYERS * 2, h=H)
            wflat = wext[:, :, :, :].rearrange("p l k c -> p (l k) c")
            for src, at in ((albc, C), (arbc, C + UV)):
                for l in range(LAYERS):
                    dve_v.tensor_tensor(hv[:, l], wext[:, l, :, 0:C], src[:, l:l + 1, :].to_broadcast([P, 2, C]), ALU.mult)
                dve.drain()
                dve_v.tensor_reduce(wflat[:, :, at:at + H], hr, AX.X, ALU.add)
                dve.drain()
            dve_v.tensor_scalar(wflat[:, :, C + H:C + UV], wflat[:, :, C:C + H], SLOPE, None, ALU.mult).then_inc(ext_ready, 1)

            def norm_stats(src, to):
                with dve.Fori(0, NT // 7) as i:
                    for j in range(7):
                        dve_v.bn_stats(bst[:, j, :], src(i, j))
                    dve.drain()
                    for j in range(7):
                        dve_v.bn_aggr(bag[:, j, :], bst[:, j, :])
                    dve.drain()
                    dve_v.tensor_copy(to[:, bass.ds(7 * i, 7), :], bag[:])
                    dve.drain()

            def res_tile(T):
                return res[:, bass.ds(T, 1), :].rearrange("p a c -> p (a c)")

            dve.wait_ge(x_in, 16)
            dve.wait_ge(k_in, 16)
            norm_stats(lambda i, j: res_tile(7 * i + j), mv)
            dve_v.tensor_scalar(rstd[:], mv[:, :, 1], EPS, None, ALU.add).then_inc(var_ready, 1)

            dve.wait_ge(d_in, 16)
            lo, hi = small[:, 0:CELLS], small[:, 32:32 + CELLS]
            dve_v.tensor_reduce(lo, dcell, AX.X, ALU.min)
            dve_v.tensor_reduce(hi, dcell, AX.X, ALU.max)
            top = small[:, 64:64 + NT]
            dve_v.tensor_scalar(top, base[:, 0:NT], float(P - 1), None, ALU.add)
            dve.drain()
            NC = NT * CELLS
            h1 = hit[:, 0:NC].rearrange("p (t c) -> p t c", t=NT)
            h2 = hit[:, NC:2 * NC].rearrange("p (t c) -> p t c", t=NT)
            cells = [P, NT, CELLS]
            dve_v.tensor_tensor(h1, lo.unsqueeze(1).to_broadcast(cells), top.unsqueeze(2).to_broadcast(cells), ALU.is_le)
            dve_v.tensor_tensor(h2, hi.unsqueeze(1).to_broadcast(cells), base[:, 0:NT].unsqueeze(2).to_broadcast(cells), ALU.is_ge)
            dve.drain()
            dve_v.tensor_tensor(h1, h1, h2, ALU.mult)
            dve.drain()
            fl = small[:, 128:128 + 2 * NT].rearrange("p (w t) -> p w t", w=2)
            for w, at in ((0, K_CELL), (1, K_CINV)):
                dve_v.tensor_tensor(h2, h1, kc[:, at:at + CELLS].unsqueeze(1).to_broadcast(cells), ALU.mult)
                dve.drain()
                dve_v.tensor_reduce(fl[:, w, :], h2, AX.X, ALU.max)
                dve.drain()
            dve.sem_inc(flags_ready, 1)
            dve.wait_ge(flagsT_ready, 1)
            lf = small[:, 240:244]
            dve_v.tensor_reduce(lf[0:NT, 0:1], tp[0:NT, 0:P], AX.X, ALU.max)
            dve_v.tensor_reduce(lf[0:NT, 1:2], tp[0:NT, P:2 * P], AX.X, ALU.max)
            dve.drain()
            dve_v.tensor_scalar(lf[0:NT, 0:1], lf[0:NT, 0:1], 1.0, None, ALU.max)
            dve_v.tensor_scalar(lf[0:NT, 1:2], lf[0:NT, 1:2], -1.0, float(BIG), ALU.mult, ALU.add)
            dve.drain()
            dve_v.tensor_scalar(lf[0:NT, 2:3], lf[0:NT, 0:1], -1.0, None, ALU.add)
            dve.drain()
            dve_v.tensor_tensor(lf[0:NT, 1:2], lf[0:NT, 1:2], lf[0:NT, 2:3], ALU.min)
            dve.drain()
            per = SLOT // CELL
            dve_v.tensor_tensor(lf[0:NT, 2:3], lf[0:NT, 0:1], lf[0:NT, 1:2], ALU.subtract)
            dve.drain()
            dve_v.tensor_scalar(ismall[0:NT, 0:1], lf[0:NT, 2:3], float(per - 1), None, ALU.add)
            dve_v.tensor_scalar(ismall[0:NT, 4:5], lf[0:NT, 1:2], float(CELL), None, ALU.mult)
            dve.drain()
            dve_v.tensor_scalar(ismall[0:NT, 1:2], ismall[0:NT, 0:1], per.bit_length() - 1, None, ALU.logical_shift_right)
            dve.drain()
            dve_v.tensor_copy(lf[0:NT, 3:4], ismall[0:NT, 1:2]).then_inc(slots_ready, 1)
            dve.wait_ge(sums_ready, 1)
            dve_v.tensor_copy(ismall[0:NT, 6:7], tp[0:NT, 256:257])
            dve_v.tensor_scalar(ismall[0:NT, 2:3], tp[0:NT, 257:258], -1.0, float(RING * TOTAL_MAX), ALU.mult, ALU.add)
            dve_v.tensor_scalar(ismall[0:NT, 3:4], tp[0:NT, 257:258], -1.0, None, ALU.add)
            dve.drain()
            dve_v.tensor_scalar(ismall[0:NT, 2:3], ismall[0:NT, 2:3], RING - 1, None, ALU.bitwise_and)
            dve_v.tensor_scalar(ismall[0:NT, 7:8], ismall[0:NT, 3:4], RING.bit_length() - 1, None, ALU.logical_shift_right)
            dve.drain()
            dve_v.tensor_copy(lf[0:NT, 0:1], ismall[0:NT, 2:3])
            dve.drain()
            dve_v.tensor_tensor(lf[0:NT, 0:1], lf[0:NT, 0:1], kc[0:NT, K_LAST:K_LAST + 1], ALU.mult)
            dve.drain()
            dve_v.tensor_tensor(ismall[0:NT, 5:6], lf[0:NT, 0:1], lf[0:NT, 3:4], ALU.add).then_inc(ctl_ready, 1)

            dve.wait_ge(std_ready, 1)
            dve_v.reciprocal(rstd[:], rstd[:])
            dve.drain()

            def first(T, b):
                dve.wait_ge(xn_free, T + 1)
                dve_v.tensor_scalar(xn[:, b, :], res_tile(T), mv[:, bass.ds(T, 1), 0:1].rearrange("p a b -> p (a b)"),
                                    rstd[:, bass.ds(T, 1)], ALU.subtract, ALU.mult).then_inc(xn_ready, 1)

            first(0, 0)
            with dve.Fori(0, NT // 2) as i:
                first(2 * i + 1, 1)
                first(2 * i + 2, 0)

            def normalise(T, b):
                dve.wait_ge(f_std, T + 1)
                dve_v.reciprocal(deviate, deviate)
                dve.drain()
                dve_v.tensor_scalar(xn[:, b, :], res_tile(T), bag[:, 0, 0:1], deviate, ALU.subtract, ALU.mult).then_inc(f_xn, 1)

            def largest_two(T, b):
                lgt, mx, i8 = (rt[:, b, at:at + 8] for at in (R_LOGIT, R_MAX, R_INDEX))
                dve.wait_ge(f_lg, T + 1)
                dve_v.tensor_tensor(lgt, hp[:, 0:EXPERTS], br[:], ALU.add)
                dve.drain()
                dve_v.max(mx, lgt)
                dve.drain()
                dve_v.max_index(mi8, mx, lgt)
                dve_v.tensor_tensor(rt[:, b, R_D:R_D + 1], mx[:, 0:1], mx[:, 1:2], ALU.subtract).then_inc(f_d, 1)
                dve.drain()
                dve_v.tensor_copy(i8, mi8)

            def weights(T, b):
                i8, t, w12 = rt[:, b, R_INDEX:R_INDEX + 8], rt[:, b, R_T:R_T + 1], rt[:, b, R_W12:R_W12 + 2]
                wf, tmp = rt[:, b, R_W:R_W + EXPERTS], rt[:, b, R_LOGIT:R_LOGIT + EXPERTS]
                dve.wait_ge(f_t, T + 1)
                dve_v.tensor_scalar(w12[:, 0:1], t, 0.5, 0.5, ALU.mult, ALU.add)
                dve_v.tensor_scalar(w12[:, 1:2], t, -0.5, 0.5, ALU.mult, ALU.add)
                dve.drain()
                dve_v.tensor_scalar(wf, iota[:, 0:EXPERTS], i8[:, 0:1], w12[:, 0:1], ALU.is_equal, ALU.mult)
                dve_v.tensor_scalar(tmp, iota[:, 0:EXPERTS], i8[:, 1:2], w12[:, 1:2], ALU.is_equal, ALU.mult)
                dve.drain()
                dve_v.tensor_tensor(wf, wf, tmp, ALU.add).then_inc(f_w, 1)

            def expert_tile(T, b, turn, following):
                dve.wait_ge(f_out[b], 16 * turn)
                dve.wait_ge(f_b2, T + 1)
                dve_v.tensor_tensor(yacc[:, b, :], res_tile(T), tp[:, C:2 * C], ALU.add)
                dve.drain()
                for e in range(EXPERTS):
                    dve.wait_ge(f_y, EXPERTS * T + e + 1)
                    dve_v.scalar_tensor_tensor(yacc[:, b, :], y_psum[e % 2][:, 0:C], rt[:, b, R_W + e:R_W + e + 1],
                                               yacc[:, b, :], ALU.mult, ALU.add).then_inc(f_yd, 1)
                    dve.drain()
                    if following and e == 0:
                        normalise(T + 1, 1 - b)
                    if following and e == 3:
                        largest_two(T + 1, 1 - b)
                    if following and e == 4:
                        weights(T + 1, 1 - b)
                dve.sem_inc(f_acc, 1)

            def exact_maxima(l):
                dve.sem_inc(seg_free[l], 1)
                with dve.If(exact_asked(dve, l) > 0), dve.Fori(0, NT) as T:
                    n_T, before = tile_ctl(dve, T)
                    dve_v.memset(seg, LOW)
                    with dve.Fori(0, n_T) as k:
                        dve.wait_ge(seg_rows[l], 16 * CH * (before + k + 1))
                        dve_v.tensor_scalar(dl[:], meta[:, 0, :, 1:2].rearrange("p c w -> p (c w)"),
                                            base[:, bass.ds(T, 1)], None, ALU.subtract)
                        dve.drain()
                        for c in range(CH):
                            dve_v.tensor_scalar(sel[:, c, :], iota, dl[:, c:c + 1], LOW, ALU.not_equal, ALU.mult)
                        dve.drain()
                        for c in range(CH):
                            for h in range(H):
                                dve_v.scalar_tensor_tensor(seg[:, h, :], sel[:, c, :], gat[:, 0, c, MSG + h:MSG + h + 1],
                                                           seg[:, h, :], ALU.add, ALU.max)
                            dve.drain()
                        dve.sem_inc(seg_free[l], 1)
                    dve.sem_inc(seg_max[l], 1)
                    dve.wait_ge(seg_turned[l], T + 1)
                    for b in range(2):
                        dve_v.tensor_reduce(small[:, 96 + b * H // 2:96 + (b + 1) * H // 2],
                                            bank[6 + b][:, :].rearrange("p (h e) -> p h e", h=H // 2), AX.X, ALU.max)
                    dve.drain()
                    dve_v.tensor_copy(uv[:, bass.ds(T, 1), 0:H].rearrange("p a h -> p (a h)"), small[:, 96:96 + H])
                    dve.drain()

            def reference_logits(l):
                ext = eler[:, :, :].rearrange("p t c -> p c t")
                dve_v.tensor_reduce(small[:, 0:H], ext[:, 0:H, :], AX.X, ALU.max)
                dve_v.tensor_reduce(small[:, H:2 * H], ext[:, 0:H, :], AX.X, ALU.min)
                dve.drain()
                dve_v.tensor_scalar(small[:, H:2 * H], small[:, H:2 * H], -1.0, None, ALU.mult)
                dve.drain()
                dve.sem_inc(extremes, 1)
                dve.wait_ge(extremesT, l + 1)
                dve_v.tensor_reduce(small[0:2 * H, 16:17], tp[0:2 * H, 0:P], AX.X, ALU.max)
                dve.drain()
                dve_v.tensor_scalar(small[0:2 * H, 32:48], ident[0:2 * H, 0:2 * H], small[0:2 * H, 16:17], None, ALU.mult)
                dve.drain()
                dve.sem_inc(spread, 1)
                dve.wait_ge(spread_done, l + 1)
                dve_v.tensor_copy(small[:, 64:80], tp[:, 0:2 * H])
                dve.drain()
                dve_v.tensor_tensor(small[:, 80:80 + H], small[:, 64:64 + H], small[:, 64 + H:80], ALU.add)
                dve_v.tensor_copy(uv[:, :, 0:H], small[:, 64:64 + H].unsqueeze(1).to_broadcast([P, NT, H]))
                dve.drain()
                dve_v.tensor_reduce(small[:, 88:89], small[:, 80:80 + H], AX.X, ALU.max)
                dve.drain()
                dve_v.tensor_scalar(span_flag, small[0:1, 88:89], SAFE, None, ALU.is_gt).then_inc(span_ready, 1)
                exact_maxima(l)
                er = eler[:, :, 2 * H:3 * H]
                u, v = uv[:, :, 0:H], uv[:, :, H:UV]
                hb = [P, NT, H]
                dve_v.tensor_tensor(u, u, er, ALU.add)
                dve.drain()
                dve_v.tensor_scalar(v, u, SLOPE, None, ALU.mult)
                dve.drain()
                c = hit[:, 0:NT * H].rearrange("p (t h) -> p t h", h=H)
                dve_v.tensor_tensor(c, u, v, ALU.max)
                dve.drain()
                dve_v.tensor_tensor(u, er, c, ALU.subtract)
                dve_v.tensor_scalar(v, er, SLOPE, None, ALU.mult)
                dve.drain()
                dve_v.tensor_tensor(v, v, c, ALU.subtract)
                dve.drain()
                flat = uv[:, :, :].rearrange("p t c -> p (t c)")
                rest = hit[:, 1024:1024 + NT * UV]
                part = [uvb[:, i, 0:NT, :].rearrange("p t c -> p (t c)") for i in range(3)]
                dve_v.tensor_copy(part[0], flat)
                dve.drain()
                dve_v.tensor_tensor(rest, flat, part[0], ALU.subtract)
                dve.drain()
                dve_v.tensor_copy(part[1], rest)
                dve.drain()
                dve_v.tensor_tensor(rest, rest, part[1], ALU.subtract)
                dve.drain()
                dve_v.tensor_copy(part[2], rest).then_inc(uvb_ready, 1)

            dve_v.memset(uvb[:, :, NT, :], 0.0)
            for l in range(LAYERS):
                dve.wait_ge(hp_free[l], NT + (2 if l == 0 else 1))
                reference_logits(l)
                dve.drain()
                dve.sem_inc(slot_free[l], RING - 1)
                dve.sem_inc(acc_free[l], 1)
                dve.wait_ge(ctl_in, 16)
                if l == 1:
                    dve.sem_inc(o_free, 1)
                if l == 0:
                    dve.wait_ge(late_in, 16 * LATE)
                    dve_v.tensor_tensor(b_bc[:, 2, :], b_bc[:, 2, :], bproj[:], ALU.add)

                def selectT(n, T):
                    dve.wait_ge(meta_ready[l], n + 1)
                    dve_v.tensor_scalar(selT[:, :, :], dstb[:, bass.ds(n % RING, 1), :].rearrange("p a (e c) -> p (a c) e", c=CH),
                                        node[:, bass.ds(T, 1)], None, ALU.is_equal).then_inc(selT_ready[l], 1)

                def place(n, T):
                    if not isinstance(n, int):
                        dve.wait_ge(dl_read[l], n)
                    dve_v.tensor_scalar(dl[:], meta[:, bass.ds(n % RING, 1), :, 1:2].rearrange("p a c w -> p (a c w)"),
                                        base[:, bass.ds(T, 1)], None, ALU.subtract).then_inc(slot_free[l], 1)
                    dve.drain()

                def select(n, chunks):
                    if not isinstance(n, int):
                        dve.wait_ge(agg_done[l], CH * n + chunks[-1] + 1)
                    for c in chunks:
                        last = dve_v.tensor_scalar(sel[:, c, :], iota, dl[:, c:c + 1], None, ALU.is_equal)
                    if chunks == BACK:
                        last.then_inc(dl_read[l], 1)

                selectT(0, 0)
                place(0, 0)
                select(0, FRONT)
                dve.sem_inc(agg_done[l], CH)

                def tile(T):
                    n_T, before = tile_ctl(dve, T)
                    with dve.Fori(0, n_T) as k:
                        n = before + k
                        rows = gat[:, bass.ds(n % RING, 1), :, :].rearrange("p a c w -> p (a c) w")
                        dve.wait_ge(uv_ready[l], n + 1)
                        dve.wait_ge(gathered[l], n + 1)
                        dve_v.tensor_tensor(lg2[:], rows[:, :, MSG:ROW],
                                            uv_p[:, 0:CH * UV].rearrange("p (c w) -> p c w", w=UV), ALU.add)
                        dve.drain()
                        dve_v.tensor_tensor(lg[:], lg2[:, :, 0:H], lg2[:, :, H:UV], ALU.max).then_inc(logit_ready[l], 1)
                        selectT(n + 1, next_tile(T, k, n_T))
                        select(n, BACK)
                        dve.wait_ge(ex_ready[l], n + 1)
                        for c in range(CH):
                            last = dve_v.tensor_tensor(
                                by_head(msg[:, c, :]), by_head(rows[:, c, 0:MSG]),
                                ex[:, c, :].unsqueeze(2).to_broadcast([P, H, D + 1]), ALU.mult).then_inc(msg_ready[l], 1)
                        place(n + 1, next_tile(T, k, n_T))
                        select(n + 1, FRONT)
                    if l == 0:
                        dve.wait_ge(v_ready, T + 1)
                        dve_v.tensor_scalar(neg[:, 0:C], bank[5][:, 0:C], 0.0, None, ALU.min)
                        dve_v.tensor_scalar(neg[:, C:2 * C], q_psum, 0.0, None, ALU.min).then_inc(neg_ready, 1)
                    if l == 1:
                        dve.wait_ge(at_psum, T + 1)
                        dve_v.tensor_scalar(den, bank[5][:, C:2 * C], 1e-6, None, ALU.max)
                        dve.drain()
                        dve_v.reciprocal(den, den)
                        dve.drain()
                        dve_v.tensor_tensor(ats, bank[5][:, 0:C], den, ALU.mult).then_inc(ats_ready, 1)
                    dve.wait_ge(acc_done[l], T + 1)
                    dve_v.tensor_scalar(rec[:], by_head(acc[:, 0:MSG])[:, :, D], 1e-37, None, ALU.max)
                    dve.drain()
                    dve_v.reciprocal(rec[:], rec[:])
                    dve.drain()
                    xo = xn[:, 0, :]
                    dve_v.tensor_tensor(xo.rearrange("p (h d) -> p h d", h=H), by_head(acc[:, 0:MSG])[:, :, 0:D],
                                        rec[:].unsqueeze(2).to_broadcast([P, H, D]), ALU.mult).then_inc(acc_free[l], 1)
                    dve.drain()
                    dve_v.tensor_tensor(xo, xo, b_bc[:, l, :], ALU.add)
                    dve.drain()
                    if l + 1 < LAYERS:
                        dve_v.scalar_tensor_tensor(xo, xo, LEAK, xo, ALU.mult, ALU.max).then_inc(xo_ready[l], 1)
                    else:
                        dve_v.tensor_tensor(res_tile(T), res_tile(T), xo, ALU.add)
                        dve.drain()
                        dve_v.bn_stats(bst[:, 0, :], res_tile(T))
                        dve.drain()
                        dve_v.bn_aggr(bag[:, 0, :], bst[:, 0, :])
                        dve.drain()
                        dve_v.tensor_scalar(deviate, bag[:, 0, 1:2], 1.0 + EPS, EPS * EPS, ALU.mult, ALU.add).then_inc(f_var, 1)
                    if l == 0:
                        dve.wait_ge(mix_free, T + 1)
                        dve.wait_ge(q_out, 16 * (T + 1))
                        dve.wait_ge(exp_ready, T + 1)
                        dve_v.tensor_copy(vx[:, C:C + 1], valid[:, bass.ds(T, 1)])
                        dve_v.scalar_tensor_tensor(kq[:, 0:C], bank[5][:, 0:C], 0.0, epos[:, 0:C], ALU.max, ALU.add)
                        dve_v.scalar_tensor_tensor(kq[:, C:2 * C], q_psum, 0.0, epos[:, C:2 * C], ALU.max, ALU.add).then_inc(kq_ready, 1)
                    if l == 1:
                        dve.wait_ge(o_psum, T + 1)
                        dve_v.tensor_tensor(res_tile(T), res_tile(T), bank[6][:, 0:C], ALU.add).then_inc(o_free, 1)
                if l + 1 < LAYERS:
                    with dve.Fori(0, NT) as T:
                        tile(T)
                else:
                    dve.sem_inc(f_yd, 2)
                    tile(0)
                    normalise(0, 0)
                    largest_two(0, 0)
                    weights(0, 0)
                    with dve.Fori(0, NT // 2) as i:
                        tile(2 * i + 1)
                        expert_tile(2 * i, 0, i + 1, True)
                        tile(2 * i + 2)
                        expert_tile(2 * i + 1, 1, i + 1, True)
                    expert_tile(NT - 1, 0, NT // 2 + 1, False)
                if l == 0:
                    dve.wait_ge(ctx_done, 1)
                    mask = kc[:, K_MASK:K_MASK + P]
                    for b in range(2):
                        dve_v.tensor_tensor(ctxm[:, b, :], bank[6 + b][:, b * P:(b + 1) * P], mask, ALU.mult)
                        dve_v.tensor_scalar(ksx[:, b, :], mask, bank[6 + b][:, C:C + 1], None, ALU.mult)
                    dve.drain()
                    dve.sem_inc(ctx_ready, 1)

        @block.tensor
        def _(pe):
            pe.wait_ge(k_in, 16)
            pe.wait_ge(flags_ready, 1)
            fl = small[:, 128:128 + 2 * NT].rearrange("p (w t) -> p w t", w=2)
            pe.matmul(tp[0:NT, 0:P], fl[:, 0, :], ident, start=True, stop=True)
            pe.matmul(tp[0:NT, P:2 * P], fl[:, 1, :], ident, start=True, stop=True).then_inc(flagsT_ready, 1)
            pe.wait_ge(slots_ready, 1)
            n_f = small[0:NT, 243:244]
            pe.matmul(tp[0:NT, 256:257], kc[0:NT, K_TRI:K_TRI + NT], n_f, start=True, stop=True)
            pe.matmul(tp[0:NT, 257:258], ones[0:NT, 0:NT], n_f, start=True, stop=True).then_inc(sums_ready, 1)
            pe.wait_ge(ctl_ready, 1)
            pe.wait_ge(ext_ready, 1)
            pe.wait_ge(zeros_ready, 2)
            pe.sem_inc(xn_free, 2)

            def project(T, l, b, hp, s_before=None):
                pe.wait_ge(hp_free[l], T + 1)
                for k in range(2):
                    last = pe.matmul(hp[:, 0:EXT], xT[:, b, k, :], wext[:, l, k, :], start=(k == 0), stop=(k == 1))
                    if k == 0 and s_before is not None:
                        last.then_inc(s_before, 1)
                last.then_inc(h_done[l], 1)

            def turn_tile(src, s_done, tp=tp):
                pe.transpose(tp[:, 0:P], src[:, 0:P], ident)
                pe.transpose(tp[:, P:2 * P], src[:, P:C], ident).then_inc(s_done, 1)

            def first(T, b):
                pe.wait_ge(xn_ready, T + 2)
                turn_tile(xn[:, 1 - b, :], xT_psum, first_tp[1 - b])
                pe.wait_ge(xT_ready, T + 1)
                project(T, 0, b, first_hp[b], xn_free)

            pe.wait_ge(xn_ready, 1)
            turn_tile(xn[:, 0, :], xT_psum, first_tp[0])
            with pe.Fori(0, NT // 2) as i:
                first(2 * i, 0)
                first(2 * i + 1, 1)
            pe.wait_ge(xT_ready, NT)
            project(NT - 1, 0, 0, first_hp[0])

            def zeros(dst, start, stop):
                return pe.matmul(dst, zb[:, 0:P], zb[:, 0:dst.shape[1]], start=start, stop=stop)

            def turn_next(T, b):
                pe.wait_ge(f_xn, T + 1)
                turn_tile(xn[:, b, :], f_tp)

            def route(T, b):
                pe.wait_ge(f_xT, 2 * (T + 1))
                for c in range(2):
                    last = pe.matmul(hp[:, 0:EXPERTS], xT[:, b, c, :], wr[:, c, :], start=(c == 0), stop=(c == 1))
                last.then_inc(f_lg, 1)

            def turn_weights(T, b):
                pe.wait_ge(f_w, T + 1)
                pe.matmul(hp[0:EXPERTS, P:2 * P], rt[:, b, R_W:R_W + EXPERTS], ident, start=True, stop=True).then_inc(f_wT_p, 1)

            def down_bias(T):
                pe.wait_ge(f_wT, T + 1)
                pe.matmul(tp[:, C:2 * C], wT, b2[:], start=True, stop=True).then_inc(f_b2, 1)

            def up(b, e):
                for k in range(HB):
                    for c in range(2):
                        last = pe.matmul(bank[5 + e % 2][:, k * P:(k + 1) * P], w1[:, e, c, k * P:(k + 1) * P],
                                         xT[:, b, c, :], start=(c == 0), stop=(c == 1))
                last.then_inc(f_h, 1)

            def down(T, e):
                pe.wait_ge(f_g, EXPERTS * T + e + 1)
                pe.wait_ge(f_yd, EXPERTS * T + e + 1)
                for k in range(HB):
                    last = pe.matmul(y_psum[e % 2][:, 0:C], gT[:, e % 2, k, :], w2[:, e, k, :],
                                     start=(k == 0), stop=(k == HB - 1))
                last.then_inc(f_y, 1)

            def expert_tile(T, b, following):
                for e in range(EXPERTS):
                    if e + 1 < EXPERTS:
                        up(b, e + 1)
                    elif following:
                        down_bias(T + 1)
                        up(1 - b, 0)
                    down(T, e)
                    if following and e == 1:
                        turn_next(T + 1, 1 - b)
                    if following and e == 3:
                        route(T + 1, 1 - b)
                    if following and e == 5:
                        turn_weights(T + 1, 1 - b)

            for l in range(LAYERS):
                pe.wait_ge(extremes, l + 1)
                pe.matmul(tp[0:2 * H, 0:P], small[:, 0:2 * H], ident, start=True, stop=True).then_inc(extremesT, 1)
                pe.wait_ge(spread, l + 1)
                pe.matmul(tp[:, 0:2 * H], ones[0:2 * H, :], small[0:2 * H, 32:48], start=True, stop=True).then_inc(spread_done, 1)

                def prepare(n, T):
                    pe.wait_ge(selT_ready[l], n + 1)
                    for c in range(CH):
                        for part in range(3):
                            last = pe.matmul(uv_p[:, c * UV:(c + 1) * UV], selT[:, c, :],
                                             uvb[:, part, bass.ds(T, 1), :].rearrange("p a b -> p (a b)"),
                                             start=(part == 0), stop=(part == 2))
                    last.then_inc(uv_ready[l], 1)

                with pe.If(exact_asked(pe, l) > 0), pe.Fori(0, NT) as T:
                    pe.wait_ge(seg_max[l], T + 1)
                    for h in range(H):
                        last = pe.transpose(bank[6 + h // 4][:, (h % 4) * P:(h % 4 + 1) * P], seg[:, h, :], ident)
                    last.then_inc(seg_turned[l], 1)

                pe.wait_ge(uvb_ready, l + 1)
                if l == 0:
                    pe.wait_ge(late_in, 16 * LATE)
                    pe.sem_inc(mix_free, 1)
                    for b in range(2):
                        zeros(bank[6 + b][:, 0:C + 1], True, False)
                prepare(0, 0)

                def tile(T):
                    n_T, before = tile_ctl(pe, T)
                    if l == 0:
                        pe.wait_ge(xnT_in, 16 * (T + 1))
                        for c in range(2):
                            pe.matmul(bank[5][:, :], xnTs[:, c, :], wkvT[:, c, :], start=(c == 0), stop=(c == 1))
                        for o in range(2):
                            for c in range(2):
                                last = pe.matmul(q_psum[:, o * P:(o + 1) * P], wqT[:, c, o * P:(o + 1) * P], xnTs[:, c, :],
                                                 start=(c == 0), stop=(c == 1))
                        last.then_inc(mix_psum, 1)
                    if l == 1:
                        pe.wait_ge(ctx_ready, 1)
                        pe.wait_ge(qT_in, 16 * (T + 1))
                        for b in range(2):
                            pe.matmul(bank[5][:, b * P:(b + 1) * P], ctxm[:, b, :], qTs[:, b, :], start=True, stop=True)
                            last = pe.matmul(bank[5][:, C + b * P:C + (b + 1) * P], ksx[:, b, :], qTs[:, b, :], start=True, stop=True)
                        last.then_inc(at_psum, 1)
                    pe.wait_ge(acc_free[l], T + 1)
                    zeros(acc[:, 0:MSG], True, False)
                    with pe.Fori(0, n_T) as k:
                        n = before + k
                        prepare(n + 1, next_tile(T, k, n_T))
                        for c in range(CH):
                            pe.wait_ge(msg_ready[l], CH * n + c + 1)
                            pe.matmul(acc[:, 0:MSG], sel[:, c, :], msg[:, c, :], start=False, stop=False).then_inc(agg_done[l], 1)
                    zeros(acc[:, 0:MSG], False, True).then_inc(acc_done[l], 1)
                    if l == 1:
                        pe.wait_ge(ats_ready, T + 1)
                        pe.wait_ge(o_free, T + 1)
                        for b in range(2):
                            last = pe.matmul(bank[6][:, 0:C], ats[:, b * P:(b + 1) * P], wpT[:, b, :], start=(b == 0), stop=(b == 1))
                        last.then_inc(o_psum, 1)
                    if l + 1 < LAYERS:
                        pe.wait_ge(xo_ready[l], T + 1)
                        turn_tile(xn[:, 0, :], xoT_psum[l])
                    if l == 0:
                        pe.wait_ge(kq_ready, T + 1)
                        for b in range(2):
                            last = pe.matmul(bank[6 + b][:, 0:C + 1], kq[:, b * P:(b + 1) * P], vx, start=False, stop=False)
                        last.then_inc(mix_free, 1)
                    if l + 1 < LAYERS:
                        pe.wait_ge(xoT_ready[l], T + 1)
                        project(T, l + 1, 0, hp)

                if l + 1 < LAYERS:
                    with pe.Fori(0, NT) as T:
                        tile(T)
                else:
                    tile(0)
                    turn_next(0, 0)
                    route(0, 0)
                    up(0, 0)
                    turn_weights(0, 0)
                    down_bias(0)
                    with pe.Fori(0, NT // 2) as i:
                        tile(2 * i + 1)
                        expert_tile(2 * i, 0, True)
                        tile(2 * i + 2)
                        expert_tile(2 * i + 1, 1, True)
                    expert_tile(NT - 1, 0, False)
                if l == 0:
                    zeros(bank[6][:, 0:C + 1], False, True)
                    zeros(bank[7][:, 0:C + 1], False, True).then_inc(ctx_done, 1)


def kernel(**inputs):
    import concourse.bacc as bacc
    from concourse.bass_utils import run_bass_kernel_spmd

    v = {n: np.asarray(x) for n, x in inputs.items()}
    edges = np.zeros((EP, 2), np.int32)
    edges[:, 1] = NO_NODE
    edges[:E, 0] = v["src"]
    edges[:E, 1] = v["dst"]
    x = np.zeros((NP, C), np.float32)
    x[:N] = v["x"]
    named = {
        "x": x, "edges": edges.reshape(-1), "dst": np.ascontiguousarray(edges[:, 1]), "consts": constants(),
        "W": v["L0_gnn_W"], "al": v["L0_gnn_al"].reshape(LAYERS, C), "ar": v["L0_gnn_ar"].reshape(LAYERS, C),
        "b": v["L0_gnn_b"], "wqT": v["L0_mix_Wq"].T, "wkvT": v["L0_mix_Wkv"].T, "wpT": v["L0_mix_Wproj"].T,
        "bproj": v["L0_mix_bproj"], "br": v["L0_ffn_br"], "Wr": v["L0_ffn_Wr"], "W1": v["L0_ffn_W1"],
        "b1": v["L0_ffn_b1"].reshape(EXPERTS * HB, P).T, "W2": v["L0_ffn_W2"], "b2": v["L0_ffn_b2"],
        "gb": np.concatenate([v["L0_ffn_gamma"].reshape(2, P), v["L0_ffn_beta"].reshape(2, P)]).T,
    }
    nc = bacc.Bacc("TRN2", target_bir_lowering=False, num_devices=1)
    arrays, aps = {}, {}
    for name, array in named.items():
        arrays[f"in_{name}"] = np.ascontiguousarray(array)
        aps[name] = nc.dram_tensor(f"in_{name}", array.shape, mybir.dt.from_np(array.dtype), kind="ExternalInput").ap()
    out = nc.dram_tensor("out_x", (NP, C), F32, kind="ExternalOutput").ap()
    build(nc, aps, out)
    nc.compile()
    r = run_bass_kernel_spmd(nc, [arrays], core_ids=[0])
    return r.results[0]["out_x"][:N]
```
